# Optimizing a Trainium2 kernel written in Bass

```python
import numpy as np
import jax
import jax.numpy as jnp

def _softmax(x, axis=-1):
    return jax.nn.softmax(x, axis=axis)

def _gelu(x):
    return jax.nn.gelu(x, approximate=True)

def _silu(x):
    return jax.nn.silu(x)

def _sigmoid(x):
    return jax.nn.sigmoid(x)

def _layernorm(x, axis=-1, eps=1e-05):
    m = jnp.mean(x, axis=axis, keepdims=True)
    v = jnp.var(x, axis=axis, keepdims=True)
    return (x - m) / jnp.sqrt(v + eps)

def _scatter_add(tgt, idx, src, axis=0):
    return tgt.at[idx].add(src)

def _segment_sum(src, seg, n):
    return jax.ops.segment_sum(src, seg, n)
kernel_name = 'mk_seq_postln_d1_jaxref_r8_c59339'

def setup_inputs(seed: int=0):
    np.random.seed(seed)
    _w = jnp.asarray

    def _L0_attn_setup():
        import jax, jax.numpy as jnp
        import numpy as np
        import math
        B, T, C = (2, 256, 256)
        N_HEAD = 16
        N_KV = 4
        GROUP = N_HEAD // N_KV
        HS = C // N_HEAD
        WINDOW = 128
        SINK = 4

        def _sliding_window_sink_mask(t):
            i = jnp.arange(t)[:, None]
            j = jnp.arange(t)[None, :]
            causal = j <= i
            band = j >= i - (WINDOW - 1)
            mask = causal & band
            mask = mask | (j < SINK)
            mask = mask & ((i >= SINK) | causal)
            return mask
        key = jax.random.key(seed)
        ks = jax.random.split(key, 5)
        s = 1.0 / math.sqrt(C)
        return {'x': jax.random.normal(ks[0], (B, T, C), dtype=jnp.float32), 'Wq': jax.random.normal(ks[1], (C, C), dtype=jnp.float32) * s, 'Wk': jax.random.normal(ks[2], (N_KV * HS, C), dtype=jnp.float32) * s, 'Wv': jax.random.normal(ks[3], (N_KV * HS, C), dtype=jnp.float32) * s, 'Wo': jax.random.normal(ks[4], (C, C), dtype=jnp.float32) * s}
    _L0_attn_in = _L0_attn_setup()

    def _L0_ffn_setup():
        import jax, jax.numpy as jnp
        import numpy as np
        import math
        B, S, D = (2, 256, 256)
        H, HD = (16, 128)
        E, I = (4, 256)
        TOP_K = 2
        ROPE_THETA = 10000.0

        def _layernorm(x, w, b):
            mu = jnp.mean(x, axis=-1, keepdims=True)
            var = jnp.mean(jnp.square(x - mu), axis=-1, keepdims=True)
            return (x - mu) * jax.lax.rsqrt(var + 1e-05) * w + b

        def _rotate_half(x):
            x1, x2 = jnp.split(x, 2, axis=-1)
            return jnp.concatenate((-x2, x1), axis=-1)

        def _attention(h, wq, bq, wk, bk, wv, bv, wo, bo):
            b, s, _ = h.shape
            q = (h @ wq + bq).reshape(b, s, H, HD).transpose(0, 2, 1, 3)
            k = (h @ wk + bk).reshape(b, s, H, HD).transpose(0, 2, 1, 3)
            v = (h @ wv + bv).reshape(b, s, H, HD).transpose(0, 2, 1, 3)
            inv_freq = 1.0 / ROPE_THETA ** (jnp.arange(0, HD, 2, dtype=jnp.float32) / HD)
            freqs = jnp.arange(s, dtype=jnp.float32)[:, None] * inv_freq[None, :]
            emb = jnp.concatenate((freqs, freqs), axis=-1)
            cos = jnp.cos(emb)[None, None]
            sin = jnp.sin(emb)[None, None]
            q = q * cos + _rotate_half(q) * sin
            k = k * cos + _rotate_half(k) * sin
            scores = jnp.einsum('bhqd,bhkd->bhqk', q, k) / math.sqrt(HD)
            causal = jnp.tril(jnp.ones((s, s), bool))
            scores = jnp.where(causal[None, None], scores, jnp.finfo(jnp.float32).min)
            probs = jax.nn.softmax(scores.astype(jnp.float32), axis=-1).astype(q.dtype)
            out = jnp.einsum('bhqk,bhkd->bhqd', probs, v)
            out = out.transpose(0, 2, 1, 3).reshape(b, s, H * HD)
            return out @ wo + bo

        def _moe(h, w_gate, we1, be1, we2, be2):
            b, s, d = h.shape
            x = h.reshape(-1, d)
            t = x.shape[0]
            raw = jax.nn.softmax(x @ w_gate, axis=-1)
            top_vals, top_idx = jax.lax.top_k(raw, TOP_K)
            w = jax.nn.softmax(top_vals, axis=-1)
            comb = jnp.zeros((t, E), x.dtype).at[jnp.arange(t)[:, None], top_idx].add(w)
            hmid = jax.nn.gelu(jnp.einsum('td,edi->tei', x, we1) + be1[None], approximate=False)
            eout = jnp.einsum('tei,eid->ted', hmid, we2) + be2[None]
            out = jnp.einsum('te,ted->td', comb, eout)
            return out.reshape(b, s, d)
        key = jax.random.key(seed)
        ks = jax.random.split(key, 20)
        s = 0.02
        p = {'hidden_states': jax.random.normal(ks[0], (B, S, D), jnp.float32), 'wq': jax.random.normal(ks[1], (D, H * HD), jnp.float32) * s, 'bq': jnp.zeros((H * HD,), jnp.float32), 'wk': jax.random.normal(ks[2], (D, H * HD), jnp.float32) * s, 'bk': jnp.zeros((H * HD,), jnp.float32), 'wv': jax.random.normal(ks[3], (D, H * HD), jnp.float32) * s, 'bv': jnp.zeros((H * HD,), jnp.float32), 'wo': jax.random.normal(ks[4], (H * HD, D), jnp.float32) * s, 'bo': jnp.zeros((D,), jnp.float32), 'ln1_w': jnp.ones((D,), jnp.float32), 'ln1_b': jnp.zeros((D,), jnp.float32), 'ln2_w': jnp.ones((D,), jnp.float32), 'ln2_b': jnp.zeros((D,), jnp.float32), 'w_gate': jax.random.normal(ks[5], (D, E), jnp.float32) * s, 'we1': jax.random.normal(ks[6], (E, D, I), jnp.float32) * s, 'be1': jnp.zeros((E, I), jnp.float32), 'we2': jax.random.normal(ks[7], (E, I, D), jnp.float32) * s, 'be2': jnp.zeros((E, D), jnp.float32)}
        return p
    _L0_ffn_in = _L0_ffn_setup()
    _d = {'L0_attn_x': _L0_attn_in['x'], 'L0_attn_Wq': _L0_attn_in['Wq'], 'L0_attn_Wk': _L0_attn_in['Wk'], 'L0_attn_Wv': _L0_attn_in['Wv'], 'L0_attn_Wo': _L0_attn_in['Wo'], 'L0_ffn_wq': _L0_ffn_in['wq'], 'L0_ffn_bq': _L0_ffn_in['bq'], 'L0_ffn_wk': _L0_ffn_in['wk'], 'L0_ffn_bk': _L0_ffn_in['bk'], 'L0_ffn_wv': _L0_ffn_in['wv'], 'L0_ffn_bv': _L0_ffn_in['bv'], 'L0_ffn_wo': _L0_ffn_in['wo'], 'L0_ffn_bo': _L0_ffn_in['bo'], 'L0_ffn_ln1_w': _L0_ffn_in['ln1_w'], 'L0_ffn_ln1_b': _L0_ffn_in['ln1_b'], 'L0_ffn_ln2_w': _L0_ffn_in['ln2_w'], 'L0_ffn_ln2_b': _L0_ffn_in['ln2_b'], 'L0_ffn_w_gate': _L0_ffn_in['w_gate'], 'L0_ffn_we1': _L0_ffn_in['we1'], 'L0_ffn_be1': _L0_ffn_in['be1'], 'L0_ffn_we2': _L0_ffn_in['we2'], 'L0_ffn_be2': _L0_ffn_in['be2']}
    _x0 = _d['L0_attn_x']
    _d['L0_attn_x'] = jax.random.normal(jax.random.fold_in(jax.random.key(seed), 1), (8, 256, 256), dtype=_x0.dtype)
    del _x0
    return _d

def reference(L0_attn_x, L0_attn_Wq, L0_attn_Wk, L0_attn_Wv, L0_attn_Wo, L0_ffn_wq, L0_ffn_bq, L0_ffn_wk, L0_ffn_bk, L0_ffn_wv, L0_ffn_bv, L0_ffn_wo, L0_ffn_bo, L0_ffn_ln1_w, L0_ffn_ln1_b, L0_ffn_ln2_w, L0_ffn_ln2_b, L0_ffn_w_gate, L0_ffn_we1, L0_ffn_be1, L0_ffn_we2, L0_ffn_be2):

    def _L0_attn_ref(x, Wq, Wk, Wv, Wo):
        import jax, jax.numpy as jnp
        import numpy as np
        import math
        B, T, C = (2, 256, 256)
        N_HEAD = 16
        N_KV = 4
        GROUP = N_HEAD // N_KV
        HS = C // N_HEAD
        WINDOW = 128
        SINK = 4

        def _sliding_window_sink_mask(t):
            i = jnp.arange(t)[:, None]
            j = jnp.arange(t)[None, :]
            causal = j <= i
            band = j >= i - (WINDOW - 1)
            mask = causal & band
            mask = mask | (j < SINK)
            mask = mask & ((i >= SINK) | causal)
            return mask
        b, t, c = x.shape
        q = (x @ Wq.T).reshape(b, t, N_HEAD, HS).transpose(0, 2, 1, 3)
        q = q.reshape(b, N_KV, GROUP, t, HS)
        k = (x @ Wk.T).reshape(b, t, N_KV, HS).transpose(0, 2, 1, 3)
        v = (x @ Wv.T).reshape(b, t, N_KV, HS).transpose(0, 2, 1, 3)
        scale = 1.0 / math.sqrt(HS)
        att = jnp.einsum('bkgqd,bkjd->bkgqj', q, k) * scale
        mask = _sliding_window_sink_mask(t)
        att = jnp.where(mask[None, None, None, :, :], att, -jnp.inf)
        att = jax.nn.softmax(att, axis=-1)
        y = jnp.einsum('bkgqj,bkjd->bkgqd', att, v)
        y = y.reshape(b, N_HEAD, t, HS).transpose(0, 2, 1, 3).reshape(b, t, c)
        return y @ Wo.T

    def _L0_ffn_ref(hidden_states, wq, bq, wk, bk, wv, bv, wo, bo, ln1_w, ln1_b, ln2_w, ln2_b, w_gate, we1, be1, we2, be2):
        import jax, jax.numpy as jnp
        import numpy as np
        import math
        B, S, D = (2, 256, 256)
        H, HD = (16, 128)
        E, I = (4, 256)
        TOP_K = 2
        ROPE_THETA = 10000.0

        def _layernorm(x, w, b):
            mu = jnp.mean(x, axis=-1, keepdims=True)
            var = jnp.mean(jnp.square(x - mu), axis=-1, keepdims=True)
            return (x - mu) * jax.lax.rsqrt(var + 1e-05) * w + b

        def _rotate_half(x):
            x1, x2 = jnp.split(x, 2, axis=-1)
            return jnp.concatenate((-x2, x1), axis=-1)

        def _attention(h, wq, bq, wk, bk, wv, bv, wo, bo):
            b, s, _ = h.shape
            q = (h @ wq + bq).reshape(b, s, H, HD).transpose(0, 2, 1, 3)
            k = (h @ wk + bk).reshape(b, s, H, HD).transpose(0, 2, 1, 3)
            v = (h @ wv + bv).reshape(b, s, H, HD).transpose(0, 2, 1, 3)
            inv_freq = 1.0 / ROPE_THETA ** (jnp.arange(0, HD, 2, dtype=jnp.float32) / HD)
            freqs = jnp.arange(s, dtype=jnp.float32)[:, None] * inv_freq[None, :]
            emb = jnp.concatenate((freqs, freqs), axis=-1)
            cos = jnp.cos(emb)[None, None]
            sin = jnp.sin(emb)[None, None]
            q = q * cos + _rotate_half(q) * sin
            k = k * cos + _rotate_half(k) * sin
            scores = jnp.einsum('bhqd,bhkd->bhqk', q, k) / math.sqrt(HD)
            causal = jnp.tril(jnp.ones((s, s), bool))
            scores = jnp.where(causal[None, None], scores, jnp.finfo(jnp.float32).min)
            probs = jax.nn.softmax(scores.astype(jnp.float32), axis=-1).astype(q.dtype)
            out = jnp.einsum('bhqk,bhkd->bhqd', probs, v)
            out = out.transpose(0, 2, 1, 3).reshape(b, s, H * HD)
            return out @ wo + bo

        def _moe(h, w_gate, we1, be1, we2, be2):
            b, s, d = h.shape
            x = h.reshape(-1, d)
            t = x.shape[0]
            raw = jax.nn.softmax(x @ w_gate, axis=-1)
            top_vals, top_idx = jax.lax.top_k(raw, TOP_K)
            w = jax.nn.softmax(top_vals, axis=-1)
            comb = jnp.zeros((t, E), x.dtype).at[jnp.arange(t)[:, None], top_idx].add(w)
            hmid = jax.nn.gelu(jnp.einsum('td,edi->tei', x, we1) + be1[None], approximate=False)
            eout = jnp.einsum('tei,eid->ted', hmid, we2) + be2[None]
            out = jnp.einsum('te,ted->td', comb, eout)
            return out.reshape(b, s, d)
        a = _attention(_layernorm(hidden_states, ln1_w, ln1_b), wq, bq, wk, bk, wv, bv, wo, bo)
        h = hidden_states + a
        m = _moe(_layernorm(h, ln2_w, ln2_b), w_gate, we1, be1, we2, be2)
        return h + m
    x = L0_attn_x
    x = _layernorm(x + _L0_attn_ref(x, L0_attn_Wq, L0_attn_Wk, L0_attn_Wv, L0_attn_Wo), axis=-1)
    x = _layernorm(x + _L0_ffn_ref(x, L0_ffn_wq, L0_ffn_bq, L0_ffn_wk, L0_ffn_bk, L0_ffn_wv, L0_ffn_bv, L0_ffn_wo, L0_ffn_bo, L0_ffn_ln1_w, L0_ffn_ln1_b, L0_ffn_ln2_w, L0_ffn_ln2_b, L0_ffn_w_gate, L0_ffn_we1, L0_ffn_be1, L0_ffn_we2, L0_ffn_be2), axis=-1)
    return x

_drawn_inputs = setup_inputs


def setup_inputs(seed=0):
    import zlib

    import numpy as np

    out = dict(_drawn_inputs(seed))
    spreads = {'L0_ffn_bq': (0.0, 0.8),
     'L0_ffn_bk': (0.0, 0.8),
     'L0_ffn_bv': (0.0, 0.1),
     'L0_ffn_bo': (0.0, 0.1),
     'L0_ffn_ln1_w': (1.0, 0.6),
     'L0_ffn_ln1_b': (0.0, 0.535),
     'L0_ffn_ln2_w': (1.0, 0.6),
     'L0_ffn_ln2_b': (0.0, 0.742),
     'L0_ffn_be1': (0.0, 0.8),
     'L0_ffn_be2': (0.0, 0.1)}
    factors = {'L0_ffn_wq': 8.0, 'L0_ffn_wk': 8.0, 'L0_ffn_we1': 2.766}
    for name, (base, spread) in spreads.items():
        noise = np.random.default_rng([zlib.crc32(name.encode()), seed]).standard_normal(out[name].shape)
        drawn = base * np.exp(spread * noise) if base else spread * noise
        out[name] = jnp.asarray(drawn.astype(out[name].dtype))
    for name, factor in factors.items():
        out[name] = (out[name] * factor).astype(out[name].dtype)
    return out
```

```python
from contextlib import ExitStack

import numpy as np

import concourse.bass as bass
from concourse import mybir

F32 = mybir.dt.float32
F32R = mybir.dt.float32r
I32 = mybir.dt.int32
ALU = mybir.AluOpType
ACT = mybir.ActivationFunctionType
AX = mybir.AxisListType

P = 128
NB, T, C = 8, 256, 256
TT, KC = T // P, C // P
H = 16
HSA, KVA = 16, 4
WINDOW, SINK = 128, 4
HSB = 128
E, TOPK = 4, 2
EPS = 1e-5
ROPE_THETA = 10000.0
MASKED = -1.0e30
REP = 4
RSQRT_GUESS = 0x5F3759DF
WCH = 384
QKVW = 3 * KC * H * HSB

CONSTS = {}
_at = 0
for _name, _n in (("ident", P), ("mask_b", 3 * P), ("cos", T), ("sin", T), ("before", E * E),
                  ("mask_a", 3 * P), ("qneg", 1), ("kneg", 1)):
    CONSTS[_name] = (_at, _at + _n)
    _at += _n
NCONST = _at
NSHARED = CONSTS["before"][1]

COLS = {}
_at = 0
for _name, _n in (("bq", H), ("bk", H), ("bv", H), ("ln1_w", KC), ("ln1_b", KC), ("ln2_w", KC),
                  ("ln2_b", KC), ("be1", E * KC), ("w_gate", KC * E)):
    COLS[_name] = (_at, _at + _n)
    _at += _n
NCOLS = _at
ROWS = {"bo": (0, C), "be2": (C, C + E * C)}
NROWS = C + E * C


def const(consts, name, base=0):
    a, b = (at - base for at in CONSTS[name])
    return consts[:, a:b]


def walk_batches(eng, body):
    body(0)
    with eng.Fori(1, NB - 1) as b:
        body(b)
    body(NB - 1)


def is_first(b):
    return isinstance(b, int) and b == 0


def is_last(b):
    return isinstance(b, int) and b == NB - 1


def live(b, k):
    return not (is_first(b) and k < 0) and not (is_last(b) and k >= H)


def nth(b, per, k):
    return b * per + (k + 1)


def wait_nth(eng, sem, b, per, k):
    if not (isinstance(b, int) and b * per + k < 0):
        eng.wait_ge(sem, nth(b, per, k))


def hold(eng, passed):
    eng.sem_inc(passed, 1)


def flat(ap):
    return ap.rearrange("p a b -> p (a b)")


LN_COUNTS = (2, 2, 1, 1) + (1,) * 9 + (2,)
LN_STAGES, LN_STEPS = len(LN_COUNTS), sum(LN_COUNTS)


def layernorm_stage(dve, stage, b, src, dst, ln, done, dve_passed):
    stats, mv, work = ln
    var, y, t = (work[:, i, :] for i in range(3))
    if stage > 0:
        dve.wait_ge(done, nth(b, LN_STEPS, sum(LN_COUNTS[:stage]) - 1))
    if stage == 0:
        for tt in range(TT):
            dve.bn_stats(stats[:, tt, :], src[:, tt, :]).then_inc(done, 1)
    elif stage == 1:
        hold(dve, dve_passed)
        for tt in range(TT):
            dve.bn_aggr(mv[:, tt, :], stats[:, tt, :]).then_inc(done, 1)
    elif stage == 2:
        dve.tensor_scalar(var, mv[:, :, 1], EPS, None, ALU.add).then_inc(done, 1)
    elif stage == 3:
        dve.tensor_scalar(y.bitcast(I32), var.bitcast(I32), -0.5, float(RSQRT_GUESS), ALU.mult, ALU.add)\
           .then_inc(done, 1)
    elif stage == LN_STAGES - 1:
        for tt in range(TT):
            dve.tensor_scalar(dst[:, tt, :], src[:, tt, :], mv[:, tt, 0:1], y[:, tt:tt + 1],
                              ALU.subtract, ALU.mult).then_inc(done, 1)
    elif stage % 3 == 1:
        dve.tensor_tensor(t, y, y, ALU.mult).then_inc(done, 1)
    elif stage % 3 == 2:
        dve.scalar_tensor_tensor(out=t, in0=t, scalar=-0.5, in1=var, op0=ALU.mult, op1=ALU.mult).then_inc(done, 1)
    else:
        dve.scalar_tensor_tensor(out=y, in0=t, scalar=1.5, in1=y, op0=ALU.add, op1=ALU.mult).then_inc(done, 1)


def three_passes(pe, out, lhs_hi, lhs_lo, rhs_hi, rhs_lo, start, stop):
    pe.matmul(out, lhs_lo, rhs_hi, start=start, stop=False, skip_group_check=True)
    pe.matmul(out, lhs_hi, rhs_lo, start=False, stop=False, skip_group_check=True)
    return pe.matmul(out, lhs_hi, rhs_hi, start=False, stop=stop, skip_group_check=True)


def layer_a(nc, x, w_attn, w_out, consts_dram, w_qkv, x1, w_hi, w_lo, consts):
    VC, KCOLS, QCOLS = KVA * HSA, KVA * P, H * HSA * REP
    SCALE = HSA ** -0.5
    LAG_T, LAG_COPY, LAG_PV = 3, 4, 6
    TAIL_STEPS = 16
    NPT = 4
    LN_AT = LAG_PV + 3
    SPLIT = (0, 4, 5, 9)
    NCH = len(SPLIT)
    NPB = 4
    HPT = P // HSA

    with ExitStack() as ctx:
        def sb(name, shape, dt=F32):
            return ctx.enter_context(nc.sbuf_tensor("a_" + name, shape, dt))

        def bank(name):
            return ctx.enter_context(nc.psum_tensor("a_" + name, [P, 512], F32))

        def sem(name):
            return ctx.enter_context(nc.semaphore("a_" + name))

        a_consts = sb("consts", [P, NCONST - NSHARED])
        w_raw = sb("w_raw", [P, KC, 2 * VC + H * HSA])
        wo_raw = sb("wo_raw", [P, KC, C])
        wq_hi, wq_lo = (sb(n, [P, KC, QCOLS], F32R) for n in ("wq_hi", "wq_lo"))
        wk_hi, wk_lo = (sb(n, [P, KC, KCOLS], F32R) for n in ("wk_hi", "wk_lo"))
        wv_hi, wv_lo = (sb(n, [P, KC, T], F32R) for n in ("wv_hi", "wv_lo"))
        wo_hi, wo_lo = (sb(n, [P, KC, C], F32R) for n in ("wo_hi", "wo_lo"))
        xs = sb("xs", [P, TT, C])
        xr = sb("xr", [P, TT, C])
        xt_hi, xt_lo = (sb(n, [P, KC, T], F32R) for n in ("xt_hi", "xt_lo"))
        part_hi = [sb(f"part_hi{i}", [P, 2, T], F32R) for i in range(2)]
        q_stack = sb("q_stack", [P, H // 2, T], F32R)
        k_stack = [sb(f"k_stack{i}", [P, KVA, T], F32R) for i in range(2)]
        v_sb = sb("v_sb", [P, TT, KVA, HSA])
        ZW = 2 * P - HSA
        v_pad = sb("v_pad", [P, TT, KVA, ZW])
        probs = [sb(f"probs{i}", [P, 3 * P]) for i in range(NPB)]
        neg_max = sb("neg_max", [P, NPB, 2])
        row_max = sb("row_max", [P, NPB, 2])
        row_sum = sb("row_sum", [P, NPB, 2])
        row_inv = sb("row_inv", [P, NPB, 2])
        pt_sb = [sb(f"pt_sb{i}", [P, 3 * P]) for i in range(NPT)]
        yt_hi, yt_lo = (sb(n, [P, KC, T], F32R) for n in ("yt_hi", "yt_lo"))
        res = sb("res", [P, TT, C])
        ln = sb("stats", [P, TT, 6]), sb("mv", [P, TT, 2]), sb("work", [P, 3, TT])
        stage = [sb(f"stage{i}", [P, WCH]) for i in range(NCH)]

        s_bank = [bank(f"scores{i}") for i in range(2)]
        t_bank = [bank(f"p_t{i}") for i in range(2)]
        o_bank = [bank(f"o_t{i}") for i in range(2)]
        p_bank = [bank(f"proj{i}") for i in range(2)]
        y_bank = p_bank[1]

        consts_in, w_in = sem("consts_in"), sem("w_in")
        x_in, xr_in = sem("x_in"), sem("xr_in")
        stage_in = [sem(f"stage_in{i}") for i in range(NCH)]
        w_split, w_split_hi, zeroed = sem("w_split"), sem("w_split_hi"), sem("zeroed")
        xt_done, xt_hi_done, xt_lo_done = sem("xt_done"), sem("xt_hi_done"), sem("xt_lo_done")
        proj_done, part_hi_done = sem("proj_done"), sem("part_hi_done")
        q_done, k_done, v_done, v_pad_done = sem("q_done"), sem("k_done"), sem("v_done"), sem("v_pad_done")
        scores_done, masked, neg_done = sem("scores_done"), sem("masked"), sem("neg_done")
        exp_done, inv_done, probs_done = sem("exp_done"), sem("inv_done"), sem("probs_done")
        pt_done, pt_sb_act, pt_sb_dve = sem("pt_done"), sem("pt_sb_act"), sem("pt_sb_dve")
        pv_done, yt_hi_done, yt_lo_done = sem("pv_done"), sem("yt_hi_done"), sem("yt_lo_done")
        y_done, res_done, ln_done, x1_out = sem("y_done"), sem("res_done"), sem("ln_done"), sem("x1_out")
        dve_passed, pool_passed = sem("dve_passed"), sem("pool_passed")
        stage_hi, stage_lo = sem("stage_hi"), sem("stage_lo")

        x_view = x.rearrange("b (t p) c -> b p t c", p=P)
        x1_view = x1.rearrange("b (t p) c -> b p t c", p=P)
        ident = const(consts, "ident")
        mask = const(a_consts, "mask_a", NSHARED)

        def wv_raw(k):
            return w_raw[:, k, 0:VC].unsqueeze(1).broadcast_to([P, T // VC, VC])

        def wk_raw(k):
            return w_raw[:, k, VC:2 * VC].rearrange("p (g d) -> p g d", d=HSA).unsqueeze(2)\
                .broadcast_to([P, KVA, 2 * REP, HSA])

        def wq_raw(k):
            return w_raw[:, k, 2 * VC:].rearrange("p (h d) -> p h d", d=HSA).unsqueeze(2)\
                .broadcast_to([P, H, REP, HSA])

        def v_copies(part, k):
            return part[:, k, :].rearrange("p (r n) -> p r n", n=VC)

        def k_copies(part, k):
            return part[:, k, :].rearrange("p (g r d) -> p g r d", r=2 * REP, d=HSA)

        def q_copies(part, k):
            return part[:, k, :].rearrange("p (h r d) -> p h r d", r=REP, d=HSA)

        PROJ = {"K0": (0, 0), "V": (1, 1), "Q0": (2, 0), "Q1": (3, 1), "K1": (4, 0), "Q2": (5, 1), "Q3": (6, 0)}
        NPROJ = len(PROJ)
        NPART = NPROJ - 1
        part_no = {n: i for i, n in enumerate(n for n in PROJ if n != "V")}
        NEXT = {12: "K0", 13: "V", 14: "Q0", 15: "Q1"}
        OWN = {1: "K1", 2: "Q2", 6: "Q3"}

        def pieces(b, s):
            if s in NEXT and not is_last(b):
                yield NEXT[s], b + 1
            if s == -1 and not is_first(b):
                yield NEXT[H - 1], b
            if s in OWN:
                yield OWN[s], b

        def steps(b):
            return range(H + TAIL_STEPS if is_last(b) else H)

        def tail_of(b, s):
            if s >= H:
                return b, s - H
            return (None, None) if is_first(b) else (b - 1, s)

        def wait_part_read(eng, name, b):
            if name[0] == "K":
                wait_nth(eng, k_done, b, 4, 2 * int(name[1]) + 1)
            else:
                wait_nth(eng, q_done, b, 4, int(name[1]))

        def wait_bank_free(eng, name, b):
            if name == "V" or (name == "K0" and is_first(b)):
                return
            before = {"K0": ("Q3", -1), "Q0": ("K0", 0), "Q1": ("V", 0),
                      "K1": ("Q0", 0), "Q2": ("Q1", 0), "Q3": ("K1", 0)}[name]
            if before[0] == "V":
                wait_nth(eng, v_done, b, 1, 0)
            else:
                wait_part_read(eng, before[0], b + before[1])

        with nc.Block() as block:
            @block.sync
            def _(sp):
                sp.dma_start(consts[:, :], consts_dram[:, 0:NSHARED]).then_inc(consts_in, 16)
                sp.dma_start(a_consts[:, :], consts_dram[:, NSHARED:NCONST]).then_inc(consts_in, 16)
                sp.dma_start(xs[:, :, :], x_view[0]).then_inc(x_in, 16)
                sp.dma_start(w_raw[:, :, :], w_attn.rearrange("(k p) n -> p k n", p=P)).then_inc(w_in, 16)
                sp.dma_start(wo_raw[:, :, :], w_out.rearrange("(k p) n -> p k n", p=P)).then_inc(w_in, 16)

                def store_x1(tb):
                    sp.wait_ge(ln_done, nth(tb, LN_STEPS, LN_STEPS - 1))
                    sp.dma_start(x1_view[tb], res[:, :, :]).then_inc(x1_out, 16)

                def body(b):
                    for i in range(NCH):
                        if not is_first(b):
                            sp.wait_ge(stage_lo, nth(b - 1, NCH, i))
                        sp.dma_start(stage[i][:, :], w_qkv[:, bass.ds(b * (NCH * WCH) + i * WCH, WCH)])\
                          .then_inc(stage_in[i], 16)
                    if not is_last(b):
                        sp.wait_ge(xt_done, nth(b, 1, 0))
                        sp.dma_start(xs[:, :, :], x_view[b + 1]).then_inc(x_in, 16)
                    if not is_first(b):
                        sp.wait_ge(res_done, nth(b - 1, 1, 0))
                    sp.dma_start(xr[:, :, :], x_view[b]).then_inc(xr_in, 16)
                    if not is_first(b):
                        store_x1(b - 1)
                walk_batches(sp, body)
                store_x1(NB - 1)
                sp.wait_ge(x1_out, 16 * NB)

            @block.gpsimd
            def _(pool):
                for i in range(2):
                    pool.memset(k_stack[i][:, :, :].bitcast(F32), 0.0).then_inc(zeroed, 1)
                pool.memset(v_pad[:, :, :, :], 0.0).then_inc(zeroed, 1)

                def v_pad_copy(nb, half):
                    pool.wait_ge(v_done, nth(nb, 1, 0))
                    if is_first(nb):
                        pool.wait_ge(zeroed, 3)
                    else:
                        pool.wait_ge(pv_done, nth(nb - 1, H, 8 * half + 7))
                    hold(pool, pool_passed)
                    for g in (2 * half, 2 * half + 1):
                        pool.tensor_copy(v_pad[:, :, g, P - HSA:P], v_sb[:, :, g, :]).then_inc(v_pad_done, 1)

                def body(b):
                    if is_first(b):
                        v_pad_copy(0, 0)
                    for s in steps(b):
                        if live(b, s - 1):
                            pool.wait_ge(inv_done, nth(b, H, s - 1))
                            i = (s - 1) % NPB
                            for j, cols in enumerate((slice(0, P), slice(P, 3 * P))):
                                n = cols.stop - cols.start
                                ins = pool.tensor_tensor(probs[i][:, cols], probs[i][:, cols],
                                                         row_inv[:, i, j:j + 1].broadcast_to([P, n]), ALU.mult)
                            ins.then_inc(probs_done, 1)
                        if s == 7:
                            v_pad_copy(b, 1)
                        if s == 15 and not is_last(b):
                            v_pad_copy(b + 1, 0)
                walk_batches(pool, body)

            @block.scalar
            def _(act):
                act.wait_ge(w_in, 32)
                for k in range(KC):
                    act.activation(k_copies(wk_hi, k), wk_raw(k), ACT.Copy).then_inc(w_split_hi, 1)
                    act.activation(v_copies(wv_hi, k), wv_raw(k), ACT.Copy).then_inc(w_split_hi, 1)
                    act.activation(q_copies(wq_hi, k), wq_raw(k), ACT.Copy).then_inc(w_split_hi, 1)
                    act.activation(wo_hi[:, k, :], wo_raw[:, k, :], ACT.Copy).then_inc(w_split_hi, 1)

                def xt_high(nb):
                    act.wait_ge(xt_done, nth(nb, 1, 0))
                    if not is_first(nb):
                        act.wait_ge(proj_done, nth(nb - 1, NPROJ, NPROJ - 1))
                    act.activation(flat(xt_hi[:, :, :]), y_bank[:, :], ACT.Copy).then_inc(xt_hi_done, 1)

                def proj_high(name, nb):
                    n, i = PROJ[name]
                    act.wait_ge(proj_done, nth(nb, NPROJ, n))
                    if name == "V":
                        if not is_first(nb):
                            act.wait_ge(v_pad_done, nth(nb - 1, KVA, KVA - 1))
                        act.activation(v_sb[:, :, :, :].rearrange("p t g d -> p t (g d)"),
                                       p_bank[i][:, :].rearrange("p (t n) -> p t n", t=TT)[:, :, 0:VC],
                                       ACT.Copy).then_inc(v_done, 1)
                    else:
                        act.activation(flat(part_hi[i][:, :, :]), p_bank[i][:, :], ACT.Copy).then_inc(part_hi_done, 1)

                def yt_high(tb, t):
                    act.wait_ge(pv_done, nth(tb, H, HPT * t + HPT - 1))
                    if not is_first(tb):
                        act.wait_ge(y_done, nth(tb - 1, 1, 0))
                    act.activation(yt_hi[:, t, :], o_bank[t][:, 0:T], ACT.Copy).then_inc(yt_hi_done, 1)

                def body(b):
                    if is_first(b):
                        xt_high(0)
                        for name in NEXT.values():
                            proj_high(name, 0)
                    for s in steps(b):
                        if s == 11 and not is_last(b):
                            xt_high(b + 1)
                        if live(b, s - LAG_COPY) and (s - LAG_COPY) % 2 == 0:
                            k = s - LAG_COPY
                            act.wait_ge(pt_done, nth(b, H, k))
                            wait_nth(act, pv_done, b, H, k - NPT)
                            act.activation(pt_sb[k % NPT][:, :], t_bank[k % 2][:, 0:3 * P], ACT.Copy).then_inc(pt_sb_act, 1)
                        for name, nb in pieces(b, s - 1):
                            proj_high(name, nb)
                        if live(b, s):
                            i = s % NPB
                            act.wait_ge(neg_done, nth(b, H, s))
                            for j, cols in enumerate((slice(0, P), slice(P, 3 * P))):
                                ins = act.activation(probs[i][:, cols], probs[i][:, cols], ACT.Exp,
                                                     bias=neg_max[:, i, j:j + 1], scale=SCALE,
                                                     accum_out=row_sum[:, i, j:j + 1])
                            ins.then_inc(exp_done, 1)
                        if s in SPLIT:
                            i = SPLIT.index(s)
                            act.wait_ge(stage_in[i], nth(b, 16, 15))
                            act.activation(w_hi[:, bass.ds(b * (NCH * WCH) + i * WCH, WCH)], stage[i][:, :],
                                           ACT.Copy).then_inc(stage_hi, 1)
                        tb, ts = tail_of(b, s)
                        if ts == LAG_PV:
                            yt_high(tb, 1)
                        if s == LAG_PV + HPT:
                            yt_high(b, 0)
                walk_batches(act, body)

            @block.vector
            def _(dve):
                dve.wait_ge(w_in, 32)
                dve.wait_ge(consts_in, 32)
                def split_low(n, lo, raw, hi):
                    dve.wait_ge(w_split_hi, n + 1)
                    dve.tensor_tensor(lo, raw, hi.bitcast(F32), ALU.subtract).then_inc(w_split, 1)

                for k in range(KC):
                    split_low(4 * k, k_copies(wk_lo, k), wk_raw(k), k_copies(wk_hi, k))
                    split_low(4 * k + 1, v_copies(wv_lo, k), wv_raw(k), v_copies(wv_hi, k))
                    split_low(4 * k + 2, q_copies(wq_lo, k), wq_raw(k), q_copies(wq_hi, k))
                    split_low(4 * k + 3, wo_lo[:, k, :], wo_raw[:, k, :], wo_hi[:, k, :])

                def xt_low(nb):
                    dve.wait_ge(xt_hi_done, nth(nb, 1, 0))
                    dve.tensor_tensor(flat(xt_lo[:, :, :]), y_bank[:, :], flat(xt_hi[:, :, :].bitcast(F32)),
                                      ALU.subtract).then_inc(xt_lo_done, 1)

                def stack(name, nb):
                    if name == "V":
                        return
                    n, i = PROJ[name]
                    dve.wait_ge(part_hi_done, nth(nb, NPART, part_no[name]))
                    j = int(name[1])
                    if name[0] == "Q":
                        if not is_first(nb):
                            dve.wait_ge(scores_done, nth(nb - 1, H, 4 * j + 3))
                        dve.scalar_tensor_tensor(
                            out=flat(q_stack[:, 2 * j:2 * j + 2, :]), in0=flat(part_hi[i][:, :, :].bitcast(F32)),
                            scalar=const(a_consts, "qneg", NSHARED), in1=p_bank[i][:, :], op0=ALU.mult, op1=ALU.add)\
                           .then_inc(q_done, 1)
                    else:
                        if is_first(nb):
                            dve.wait_ge(zeroed, 3)
                        else:
                            dve.wait_ge(scores_done, nth(nb - 1, H, 8 * j + 7))
                        for half in range(2):
                            rows = slice(64 * half, 64 * half + 64)
                            dve.scalar_tensor_tensor(
                                out=flat(k_stack[half][rows, 2 * j:2 * j + 2, :]),
                                in0=flat(part_hi[i][rows, :, :].bitcast(F32)),
                                scalar=const(a_consts, "kneg", NSHARED)[rows, :], in1=p_bank[i][rows, :],
                                op0=ALU.mult, op1=ALU.add).then_inc(k_done, 1)

                def yt_low(tb, t):
                    dve.wait_ge(yt_hi_done, nth(tb, 2, t))
                    dve.tensor_tensor(yt_lo[:, t, :], o_bank[t][:, 0:T], yt_hi[:, t, :].bitcast(F32),
                                      ALU.subtract).then_inc(yt_lo_done, 1)

                def layernorm_part(tb, ts, half):
                    if ts is not None and LN_AT <= ts < LN_AT + LN_STAGES // 2:
                        layernorm_stage(dve, 2 * (ts - LN_AT) + half, tb, res, res, ln, ln_done, dve_passed)

                def row_inverse(b, k):
                    dve.wait_ge(exp_done, nth(b, H, k))
                    dve.reciprocal(row_inv[:, k % NPB, :], row_sum[:, k % NPB, :]).then_inc(inv_done, 1)

                def body(b):
                    if is_first(b):
                        xt_low(0)
                        for name in NEXT.values():
                            stack(name, 0)
                    for s in steps(b):
                        tb, ts = tail_of(b, s)
                        if ts == LN_AT:
                            dve.wait_ge(y_done, nth(tb, 1, 0))
                            dve.wait_ge(xr_in, nth(tb, 16, 15))
                            if not is_first(tb):
                                dve.wait_ge(x1_out, nth(tb - 1, 16, 15))
                            dve.tensor_tensor(flat(res[:, :, :]), y_bank[:, :], flat(xr[:, :, :]),
                                              ALU.add).then_inc(res_done, 1)
                            dve.wait_ge(res_done, nth(tb, 1, 0))
                        layernorm_part(tb, ts, 0)
                        if live(b, s - LAG_COPY) and (s - LAG_COPY) % 2 == 1:
                            k = s - LAG_COPY
                            dve.wait_ge(pt_done, nth(b, H, k))
                            wait_nth(dve, pv_done, b, H, k - NPT)
                            dve.tensor_copy(pt_sb[k % NPT][:, :], t_bank[k % 2][:, 0:3 * P]).then_inc(pt_sb_dve, 1)
                        if live(b, s):
                            i = s % NPB
                            wait_nth(dve, pt_done, b, H, s - NPB)
                            dve.wait_ge(scores_done, nth(b, H, s))
                            hold(dve, dve_passed)
                            for j, (dst, src) in enumerate(((slice(0, P), slice(0, P)), (slice(P, 3 * P), slice(T, 2 * T)))):
                                dve.tensor_tensor_reduce(probs[i][:, dst], s_bank[s % 2][:, src], mask[:, dst],
                                                         1.0, MASKED, ALU.add, ALU.max,
                                                         row_max[:, i, j:j + 1]).then_inc(masked, 1)
                            dve.wait_ge(masked, nth(b, 2 * H, 2 * s + 1))
                            dve.tensor_scalar(neg_max[:, i, :], row_max[:, i, :], -SCALE, None,
                                              ALU.mult).then_inc(neg_done, 1)
                        if live(b, s - 1):
                            row_inverse(b, s - 1)
                        if s == 11 and not is_last(b):
                            xt_low(b + 1)
                        for name, nb in pieces(b, s - 1):
                            stack(name, nb)
                        layernorm_part(tb, ts, 1)
                        if ts == LAG_PV:
                            yt_low(tb, 1)
                        if s == LAG_PV + HPT:
                            yt_low(b, 0)
                        if s - 1 in SPLIT:
                            i = SPLIT.index(s - 1)
                            dve.wait_ge(stage_hi, nth(b, NCH, i))
                            at = bass.ds(b * (NCH * WCH) + i * WCH, WCH)
                            dve.tensor_tensor(w_lo[:, at], stage[i][:, :], w_hi[:, at].bitcast(F32),
                                              ALU.subtract).then_inc(stage_lo, 1)
                walk_batches(dve, body)

            @block.tensor
            def _(pe):
                def transpose_x(nb):
                    pe.wait_ge(x_in, nth(nb, 16, 15))
                    if is_first(nb):
                        pe.wait_ge(consts_in, 32)
                    elif isinstance(nb, int) and nb == 1:
                        pe.wait_ge(q_done, nth(0, 4, 2))
                    else:
                        pe.wait_ge(res_done, nth(nb - 2, 1, 0))
                    for k in range(KC):
                        for tt in range(TT):
                            ins = pe.transpose(y_bank[:, k * T + tt * P:k * T + tt * P + P],
                                               xs[:, tt, k * P:k * P + P], ident)
                    ins.then_inc(xt_done, 1)

                def project(name, nb):
                    n, i = PROJ[name]
                    if is_first(nb):
                        pe.wait_ge(w_split, 2 * 4)
                    pe.wait_ge(xt_lo_done, nth(nb, 1, 0))
                    wait_bank_free(pe, name, nb)
                    for j in range(2):
                        out = p_bank[i][:, j * T:j * T + T]
                        for k in range(KC):
                            if name == "V":
                                tok = slice(j * P, j * P + P)
                                args = (xt_hi[:, k, tok], xt_lo[:, k, tok], wv_hi[:, k, :], wv_lo[:, k, :])
                            else:
                                hi, lo = (wk_hi, wk_lo) if name[0] == "K" else (wq_hi, wq_lo)
                                m = (2 * int(name[1]) + j) * P
                                args = (hi[:, k, m:m + P], lo[:, k, m:m + P], xt_hi[:, k, :], xt_lo[:, k, :])
                            ins = three_passes(pe, out, *args, start=(k == 0), stop=(k == KC - 1))
                    ins.then_inc(proj_done, 1)

                def project_out(tb):
                    pe.wait_ge(yt_lo_done, nth(tb, 2, 1))
                    pe.wait_ge(q_done, nth(tb if is_last(tb) else tb + 1, 4, 2))
                    for tt in range(TT):
                        tok = slice(tt * P, tt * P + P)
                        for k in range(KC):
                            ins = three_passes(pe, y_bank[:, tt * C:tt * C + C], yt_hi[:, k, tok], yt_lo[:, k, tok],
                                               wo_hi[:, k, :], wo_lo[:, k, :], start=(k == 0), stop=(k == KC - 1))
                    ins.then_inc(y_done, 1)

                def weigh_values(b, k):
                    h = k % H
                    t, hh, g = h // HPT, h % HPT, h * KVA // H
                    copied = (pt_sb_act, pt_sb_dve)[k % 2]
                    pe.wait_ge(copied, nth(b, H // 2, (k - k % 2) // 2))
                    if h % (H // KVA) == 0:
                        pe.wait_ge(v_pad_done, nth(b, KVA, (k - h) // H * KVA + g))
                    if hh == 0:
                        wait_nth(pe, yt_lo_done, b, 2, ((k - h) // H - 1) * 2 + t)
                    o, pt, at = o_bank[t], pt_sb[k % NPT], P - HSA - HSA * hh
                    pe.matmul(o[:, 0:T], v_pad[:, 0, g, at:at + P], pt[:, 0:T], start=(hh == 0), stop=False,
                              skip_group_check=True)
                    pe.matmul(o[:, P:T], v_pad[:, 1, g, at:at + P], pt[:, T:3 * P], start=False,
                              stop=(hh == HPT - 1), skip_group_check=True).then_inc(pv_done, 1)

                def body(b):
                    if is_first(b):
                        transpose_x(0)
                        for name in NEXT.values():
                            project(name, 0)
                    for s in steps(b):
                        if live(b, s - LAG_PV):
                            weigh_values(b, s - LAG_PV)
                        if live(b, s):
                            if s % 4 == 0:
                                pe.wait_ge(q_done, nth(b, 4, s // 4))
                            if s % 8 == 0:
                                pe.wait_ge(k_done, nth(b, 4, 2 * (s // 8) + 1))
                            wait_nth(pe, masked, b, 2 * H, 2 * (s - 2) + 1)
                            for tt in range(TT):
                                ins = pe.matmul(s_bank[s % 2][:, tt * T:tt * T + T],
                                                q_stack[:, s // 2, tt * P:tt * P + P],
                                                k_stack[s % 2][:, s * KVA // H, :], start=True, stop=True)
                            ins.then_inc(scores_done, 1)
                        if live(b, s - LAG_T):
                            k = s - LAG_T
                            pe.wait_ge(probs_done, nth(b, H, k))
                            copied = (pt_sb_act, pt_sb_dve)[k % 2]
                            if live(b, k - 2):
                                pe.wait_ge(copied, nth(b, H // 2, (k - 2 - k % 2) // 2))
                            for c in range(3):
                                ins = pe.transpose(t_bank[k % 2][:, c * P:c * P + P], probs[k % NPB][:, c * P:c * P + P], ident)
                            ins.then_inc(pt_done, 1)
                        tb, ts = tail_of(b, s)
                        if ts == LAG_PV + 2:
                            project_out(tb)
                        if s == 10 and not is_last(b):
                            transpose_x(b + 1)
                        for name, nb in pieces(b, s):
                            project(name, nb)
                walk_batches(pe, body)


def layer_b(nc, x1, w_qkv_hi, w_qkv_lo, w_out, w_moe, cols_dram, rows_dram, out, consts):
    SCALE = HSB ** -0.5
    HALF = HSB // 2
    LEAD = 3
    LAG_T, LAG_PV, LAG_O = 1, 2, 3
    TAIL_STEPS = 26
    NPB = 2
    VPAIRS = H // 2
    WO_CH = KC * T
    N_WO = H * C // WO_CH
    SEGS = (slice(0, P), slice(P, 3 * P))
    ROUTE = {9: ((), (), (0,), (1,)), 10: ((2,), (3, 4), (5, 6), (7, 8)), 11: ((9,), (10, 11), (12, 13), (14,)),
             12: ((15,), (), (), ()), 13: ((), (16,), (17, 18), (19, 20))}
    N_ROUTE = 21
    LN_P_AT, LN_H_AT, LN_O_AT = 4, 3, 20
    R_SHIFTED, R_GAP = 1, 15

    with ExitStack() as ctx:
        def sb(name, shape, dt=F32):
            return ctx.enter_context(nc.sbuf_tensor("b_" + name, shape, dt))

        def bank(name):
            return ctx.enter_context(nc.psum_tensor("b_" + name, [P, 512], F32))

        def sem(name):
            return ctx.enter_context(nc.semaphore("b_" + name))

        def ln_buffers(n):
            return sb(f"stats_{n}", [P, TT, 6]), sb(f"mv_{n}", [P, TT, 2]), sb(f"work_{n}", [P, 3, TT])

        wo_hi, wo_lo = (sb(n, [P, H, C], F32R) for n in ("wo_hi", "wo_lo"))
        w_up = sb("w_up", [P, E, KC, C])
        w_down = sb("w_down", [P, E, KC, C])
        cols, rows = sb("cols", [P, NCOLS]), sb("rows", [P, NROWS])
        xp = sb("xp", [P, TT, C])
        xt = sb("xt", [P, TT, C])
        h_sb = sb("h_sb", [P, TT, C])
        xn = sb("xn", [P, TT, C])
        mix = sb("mix", [P, TT, C])
        zp, zt = sb("zp", [P, TT, C]), sb("zt", [P, TT, C])
        ht, h2t = sb("ht", [P, KC, T]), sb("h2t", [P, KC, T])
        ht_hi, ht_lo = (sb(n, [P, KC, T], F32R) for n in ("ht_hi", "ht_lo"))
        qk = [sb(f"qk{i}", [P, 2, T]) for i in range(2)]
        qk_swap = [sb(f"qk_swap{i}", [P, 2, T]) for i in range(2)]
        qk_rot = [sb(f"qk_rot{i}", [P, 2, T]) for i in range(2)]
        v_sb = [sb(f"v_sb{i}", [P, TT, 2, HSB]) for i in range(2)]
        probs = [sb(f"probs{i}", [P, 3 * P]) for i in range(NPB)]
        neg_max, row_max, row_sum, row_inv = (
            sb(n, [P, NPB, 2]) for n in ("neg_max", "row_max", "row_sum", "row_inv"))
        pt_sb = [sb(f"pt_sb{i}", [P, 3 * P]) for i in range(2)]
        ot_hi, ot_lo = ([sb(f"{n}{i}", [P, T], F32R) for i in range(2)] for n in ("ot_hi", "ot_lo"))
        units = [sb(f"units{i}", [P, KC, T]) for i in range(2)]
        ln_p, ln_h, ln_o = (ln_buffers(n) for n in "pho")
        first, total, inv_total, second, gap, share = (sb(n, [P, TT, 1]) for n in (
            "first", "total", "inv_total", "second", "gap", "share"))
        shifted, expd, raw, rank, is_top, is_second, picked, comb = (sb(n, [P, TT, E]) for n in (
            "shifted", "expd", "raw", "rank", "is_top", "is_second", "picked", "comb"))
        above, equal = sb("above", [P, TT, E, E]), sb("equal", [P, TT, E, E])

        qk_bank, v_bank, s_bank, t_bank, o_bank, y_bank = (
            bank(n) for n in ("qk", "v", "scores", "p_t", "o_t", "y"))
        m_bank = [bank(f"moe{i}") for i in range(2)]

        params_in, moe_in = sem("params_in"), sem("moe_in")
        wo_in = [sem(f"wo_in{i}") for i in range(2)]
        wo_hi_done, wo_lo_done = sem("wo_hi_done"), sem("wo_lo_done")
        xp_in, xt_in = sem("xp_in"), sem("xt_in")
        ln_p_done, ln_h_done, ln_o_done = sem("ln_p_done"), sem("ln_h_done"), sem("ln_o_done")
        xpt_done, ht_done, ht_parts = sem("xpt_done"), sem("ht_done"), sem("ht_parts")
        qk_proj, qk_done, rope_done, rot_done = sem("qk_proj"), sem("qk_done"), sem("rope_done"), sem("rot_done")
        swap_in = [sem(f"swap_in{i}") for i in range(2)]
        v_proj, v_done = sem("v_proj"), sem("v_done")
        scores_done, masked, neg_done = sem("scores_done"), sem("masked"), sem("neg_done")
        exp_done, inv_done, probs_done = sem("exp_done"), sem("inv_done"), sem("probs_done")
        pt_done, pt_copied, pv_done = sem("pt_done"), sem("pt_copied"), sem("pv_done")
        ot_hi_done, ot_lo_done, o_proj = sem("ot_hi_done"), sem("ot_lo_done"), sem("o_proj")
        hb_done, h_done = sem("hb_done"), sem("h_done")
        h2t_psum, h2t_done, logits_psum = sem("h2t_psum"), sem("h2t_done"), sem("logits_psum")
        route, route_exp = sem("route"), sem("route_exp")
        up_done, units_done, down_done, mixed = sem("up_done"), sem("units_done"), sem("down_done"), sem("mixed")
        bias_done, sum_done, stored = sem("bias_done"), sem("sum_done"), sem("stored")
        dve_passed = sem("dve_passed")

        x1_view = x1.rearrange("b (t p) c -> b p t c", p=P)
        out_view = out.rearrange("b (t p) c -> b p t c", p=P)
        ident, mask = const(consts, "ident"), const(consts, "mask_b")
        cos = const(consts, "cos").unsqueeze(1).broadcast_to([P, 2, T])
        sin = const(consts, "sin").unsqueeze(1).broadcast_to([P, 2, T])
        before = const(consts, "before").rearrange("p (i j) -> p i j", i=E)

        def col(name, i=0):
            a = COLS[name][0] + i
            return cols[:, a:a + 1]

        def row(name, i=0):
            a = ROWS[name][0] + i * C
            return rows[:, a:a + C].unsqueeze(1).broadcast_to([P, TT, C])

        def steps(b):
            return range(-LEAD if is_first(b) else 0, H + TAIL_STEPS if is_last(b) else H)

        def tails(b, s):
            for j in range(3):
                ts = s + (j - 1) * H
                if 0 <= ts < TAIL_STEPS and not (isinstance(b, int) and b < j):
                    yield b - j, ts

        def walk(eng, body):
            body(0)
            body(1)
            with eng.Fori(2, NB - 1) as b:
                body(b)
            body(NB - 1)

        def wait_swap(eng, b, k):
            eng.wait_ge(swap_in[k % 2], b * (2 * 16 * H // 2) + 2 * 16 * (k // 2 + 1))

        with nc.Block() as block:
            @block.sync
            def _(sp):
                sp.dma_start(rows[:, :], rows_dram).then_inc(params_in, 16)
                sp.dma_start(cols[:, :], cols_dram).then_inc(params_in, 16)
                sp.dma_start(xp[:, :, :], x1_view[0]).then_inc(xp_in, 16)

                def load_w_out(c):
                    if c >= 2:
                        sp.wait_ge(wo_lo_done, c - 1)
                    sp.dma_start(flat(units[c % 2][:, :, :]), w_out[:, c * WO_CH:(c + 1) * WO_CH])\
                      .then_inc(wo_in[c % 2], 16)

                def load_w_moe():
                    n = E * KC * C
                    sp.dma_start(w_up[:, :, :, :].rearrange("p e k n -> p (e k n)"), w_moe[:, 0:n])\
                      .then_inc(moe_in, 16)
                    sp.dma_start(w_down[:, :, :, :].rearrange("p e k n -> p (e k n)"), w_moe[:, n:2 * n])\
                      .then_inc(moe_in, 16)

                def body(b):
                    for s in steps(b):
                        if live(b, s + 2):
                            k = s + 2
                            sp.wait_ge(qk_done, nth(b, 2 * H, 2 * k + 1))
                            for lo, hi in ((0, HALF), (HALF, 0)):
                                sp.dma_start(qk_swap[k % 2][lo:lo + HALF, :, :], qk[k % 2][hi:hi + HALF, :, :])\
                                  .then_inc(swap_in[k % 2], 16)
                        if is_first(b) and s + LEAD < N_WO:
                            load_w_out(s + LEAD)
                        if is_first(b) and s + LEAD == N_WO:
                            load_w_moe()
                        if s == 1 and not is_last(b):
                            sp.wait_ge(xpt_done, nth(b, 1, 0))
                            sp.dma_start(xp[:, :, :], x1_view[b + 1]).then_inc(xp_in, 16)
                        if s == 15:
                            if not is_first(b):
                                sp.wait_ge(bias_done, nth(b - 1, 2 * E, 1))
                            sp.dma_start(xt[:, :, :], x1_view[b]).then_inc(xt_in, 16)
                        for tb, ts in tails(b, s):
                            if ts == TAIL_STEPS - 1:
                                sp.wait_ge(ln_o_done, nth(tb, LN_STEPS, LN_STEPS - 1))
                                sp.dma_start(out_view[tb], mix[:, :, :]).then_inc(stored, 16)
                walk(sp, body)
                sp.wait_ge(stored, 16 * NB)

            @block.gpsimd
            def _(pool):
                def add_out_bias(tb):
                    pool.wait_ge(xt_in, nth(tb, 16, 15))
                    if is_first(tb):
                        pool.wait_ge(params_in, 32)
                    else:
                        pool.wait_ge(mixed, nth(tb - 1, E * TT, TT - 1))
                    pool.tensor_tensor(h_sb[:, :, :], xt[:, :, :], row("bo"), ALU.add).then_inc(hb_done, 1)

                def add_expert_bias(tb, e):
                    if e == 0:
                        pool.wait_ge(route, nth(tb, N_ROUTE, N_ROUTE - 1))
                        if not is_first(tb):
                            pool.wait_ge(sum_done, nth(tb - 1, 1, 0))
                    wait_nth(pool, bias_done, tb, 2 * E, 2 * e - 1)
                    pool.tensor_tensor(zt[:, :, :], row("be2", e), comb[:, :, e:e + 1].broadcast_to([P, TT, C]),
                                       ALU.mult).then_inc(bias_done, 1)
                    pool.wait_ge(bias_done, nth(tb, 2 * E, 2 * e))
                    pool.tensor_tensor(zp[:, :, :], (xt if e == 0 else zp)[:, :, :], zt[:, :, :], ALU.add)\
                        .then_inc(bias_done, 1)

                def body(b):
                    for s in steps(b):
                        if live(b, s):
                            i = s % NPB
                            pool.wait_ge(inv_done, nth(b, H, s))
                            for j, seg in enumerate(SEGS):
                                n = seg.stop - seg.start
                                ins = pool.tensor_tensor(probs[i][:, seg], probs[i][:, seg],
                                                         row_inv[:, i, j:j + 1].broadcast_to([P, n]), ALU.mult)
                            ins.then_inc(probs_done, 1)
                        if live(b, s + 2):
                            k = s + 2
                            pool.wait_ge(rope_done, nth(b, 2 * H, 2 * k + 1))
                            wait_nth(pool, scores_done, b, H, k - 2)
                            pool.tensor_tensor(qk_rot[k % 2][:, :, :], qk[k % 2][:, :, :],
                                               qk_swap[k % 2][:, :, :], ALU.add).then_inc(rot_done, 1)
                        for tb, ts in tails(b, s):
                            if ts == 1:
                                add_out_bias(tb)
                            if 14 <= ts < 14 + E:
                                add_expert_bias(tb, ts - 14)
                walk(pool, body)

            @block.scalar
            def _(act):
                def affine(dst, src, name, done):
                    for k in range(KC):
                        act.activation(dst[:, k, :], src[:, k * T:k * T + T], ACT.Identity,
                                       bias=col(name + "_b", k), scale=col(name + "_w", k)).then_inc(done, 1)

                def prepare(nb):
                    act.wait_ge(xpt_done, nth(nb, 1, 0))
                    if is_first(nb):
                        act.wait_ge(params_in, 32)
                    else:
                        act.wait_ge(ht_parts, nth(nb - 1, 2, 1))
                    affine(ht, m_bank[0], "ln1", ht_done)

                def gelu(tb, pair):
                    for e in (2 * pair, 2 * pair + 1):
                        act.wait_ge(up_done, nth(tb, E, e))
                        wait_nth(act, down_done, tb, E, e - 2)
                        for i in range(KC):
                            act.activation(units[e % 2][:, i, :], m_bank[e % 2][:, i * T:i * T + T], ACT.Gelu,
                                           bias=col("be1", KC * e + i)).then_inc(units_done, 1)

                def body(b):
                    if is_first(b):
                        prepare(0)
                    for s in steps(b):
                        if live(b, s + 2):
                            k = s + 2
                            act.wait_ge(qk_proj, nth(b, H, k))
                            wait_nth(act, rot_done, b, H, k - 2)
                            for j, name in enumerate(("bq", "bk")):
                                act.activation(qk[k % 2][:, j, :], qk_bank[:, j * T:j * T + T], ACT.Identity,
                                               bias=col(name, k % H)).then_inc(qk_done, 1)
                        if live(b, s):
                            i = s % NPB
                            act.wait_ge(neg_done, nth(b, H, s))
                            for j, seg in enumerate(SEGS):
                                ins = act.activation(probs[i][:, seg], probs[i][:, seg], ACT.Exp,
                                                     bias=neg_max[:, i, j:j + 1], scale=SCALE,
                                                     accum_out=row_sum[:, i, j:j + 1])
                            ins.then_inc(exp_done, 1)
                        if live(b, s - LAG_PV):
                            k = s - LAG_PV
                            act.wait_ge(pv_done, nth(b, H, k))
                            wait_nth(act, o_proj, b, H, k - 2)
                            act.activation(ot_hi[k % 2][:, :], o_bank[:, 0:T], ACT.Identity,
                                           bias=col("bv", k % H)).then_inc(ot_hi_done, 1)
                        if live(b, s - LAG_T):
                            k = s - LAG_T
                            act.wait_ge(pt_done, nth(b, H, k))
                            wait_nth(act, pv_done, b, H, k - 2)
                            act.activation(pt_sb[k % 2][:, :], t_bank[:, 0:3 * P], ACT.Copy).then_inc(pt_copied, 1)
                        if s % 2 == 1 and live(b, s + 1):
                            k = s + 1
                            act.wait_ge(v_proj, nth(b, VPAIRS, k // 2))
                            wait_nth(act, pv_done, b, H, k - 3)
                            act.activation(v_sb[k // 2 % 2][:, :, :, :].rearrange("p t h d -> p (t h d)"),
                                           v_bank[:, :], ACT.Copy).then_inc(v_done, 1)
                        c = s + 2
                        if is_first(b) and 0 <= c < N_WO:
                            act.wait_ge(wo_in[c % 2], 16 * (c // 2 + 1))
                            act.activation(wo_hi[:, :, :].rearrange("p h c -> p (h c)")[:, c * WO_CH:(c + 1) * WO_CH],
                                           flat(units[c % 2][:, :, :]), ACT.Copy).then_inc(wo_hi_done, 1)
                        if s == 8 and not is_last(b):
                            prepare(b + 1)
                        for tb, ts in tails(b, s):
                            if ts == 7:
                                act.wait_ge(h2t_psum, nth(tb, 1, 0))
                                affine(h2t, m_bank[0], "ln2", h2t_done)
                            if ts == 9:
                                act.wait_ge(route, nth(tb, N_ROUTE, R_SHIFTED))
                                act.activation(expd[:, :, :], shifted[:, :, :], ACT.Exp).then_inc(route_exp, 1)
                            if ts == 12:
                                act.wait_ge(route, nth(tb, N_ROUTE, R_GAP))
                                act.activation(gap[:, :, :], gap[:, :, :], ACT.Exp).then_inc(route_exp, 1)
                            if ts in (12, 16):
                                gelu(tb, (ts - 12) // 4)
                walk(act, body)

            @block.vector
            def _(dve):
                dve.wait_ge(params_in, 32)

                def split_ht(nb):
                    dve.wait_ge(ht_done, nth(nb, KC, KC - 1))
                    if not is_first(nb):
                        dve.wait_ge(qk_proj, nth(nb - 1, H, H - 1))
                        dve.wait_ge(v_proj, nth(nb - 1, VPAIRS, VPAIRS - 1))
                    dve.tensor_copy(ht_hi[:, :, :], ht[:, :, :]).then_inc(ht_parts, 1)
                    dve.wait_ge(ht_parts, nth(nb, 2, 0))
                    dve.tensor_tensor(ht_lo[:, :, :], ht[:, :, :], ht_hi[:, :, :].bitcast(F32), ALU.subtract)\
                       .then_inc(ht_parts, 1)

                def route_step(tb, n):
                    if n == 0:
                        dve.wait_ge(logits_psum, nth(tb, 1, 0))
                        if not is_first(tb):
                            dve.wait_ge(bias_done, nth(tb - 1, 2 * E, 2 * E - 1))
                    else:
                        dve.wait_ge(route, nth(tb, N_ROUTE, n - 1))
                    if n == R_SHIFTED + 1:
                        dve.wait_ge(route_exp, nth(tb, 2, 0))
                    if n == R_GAP + 1:
                        dve.wait_ge(route_exp, nth(tb, 2, 1))
                    logits = m_bank[1][:, 0:TT * E].rearrange("p (t e) -> p t e", t=TT)

                    def over_experts(ap):
                        return ap[:, :, :].broadcast_to([P, TT, E])

                    def by_row(ap):
                        return ap[:, :, :].unsqueeze(3).broadcast_to([P, TT, E, E])

                    def by_column(ap):
                        return ap[:, :, :].unsqueeze(2).broadcast_to([P, TT, E, E])

                    if n == 0:
                        ins = dve.tensor_reduce(first[:, :, 0], logits, AX.X, ALU.max)
                    elif n == 1:
                        ins = dve.tensor_tensor(shifted[:, :, :], logits, over_experts(first), ALU.subtract)
                    elif n == 2:
                        ins = dve.tensor_reduce(total[:, :, 0], expd[:, :, :], AX.X, ALU.add)
                    elif n == 3:
                        ins = dve.reciprocal(inv_total[:, :, :], total[:, :, :])
                    elif n == 4:
                        ins = dve.tensor_tensor(raw[:, :, :], expd[:, :, :], over_experts(inv_total), ALU.mult)
                    elif n == 5:
                        ins = dve.tensor_tensor(above[:, :, :, :], by_column(raw), by_row(raw), ALU.is_gt)
                    elif n == 6:
                        ins = dve.tensor_tensor(equal[:, :, :, :], by_column(raw), by_row(raw), ALU.is_equal)
                    elif n == 7:
                        ins = dve.tensor_tensor(equal[:, :, :, :], equal[:, :, :, :],
                            before.unsqueeze(1).broadcast_to([P, TT, E, E]), ALU.mult)
                    elif n == 8:
                        ins = dve.tensor_tensor(above[:, :, :, :], above[:, :, :, :], equal[:, :, :, :], ALU.add)
                    elif n == 9:
                        ins = dve.tensor_reduce(rank[:, :, :], above[:, :, :, :], AX.X, ALU.add)
                    elif n == 10:
                        ins = dve.tensor_scalar(is_top[:, :, :], rank[:, :, :], 0.0, None, ALU.is_equal)
                    elif n == 11:
                        ins = dve.tensor_scalar(is_second[:, :, :], rank[:, :, :], 1.0, None, ALU.is_equal)
                    elif n == 12:
                        ins = dve.tensor_reduce(first[:, :, 0], raw[:, :, :], AX.X, ALU.max)
                    elif n == 13:
                        ins = dve.tensor_tensor(picked[:, :, :], raw[:, :, :], is_second[:, :, :], ALU.mult)
                    elif n == 14:
                        ins = dve.tensor_reduce(second[:, :, 0], picked[:, :, :], AX.X, ALU.add)
                    elif n == 15:
                        ins = dve.tensor_tensor(gap[:, :, :], second[:, :, :], first[:, :, :], ALU.subtract)
                    elif n == 16:
                        ins = dve.tensor_scalar(share[:, :, :], gap[:, :, :], 1.0, None, ALU.add)
                    elif n == 17:
                        ins = dve.reciprocal(share[:, :, :], share[:, :, :])
                    elif n == 18:
                        ins = dve.tensor_tensor(picked[:, :, :], is_second[:, :, :], over_experts(gap), ALU.mult)
                    elif n == 19:
                        ins = dve.tensor_tensor(picked[:, :, :], picked[:, :, :], is_top[:, :, :], ALU.add)
                    elif n == 20:
                        ins = dve.tensor_tensor(comb[:, :, :], picked[:, :, :], over_experts(share), ALU.mult)
                    ins.then_inc(route, 1)

                def mix_expert(tb, e):
                    dve.wait_ge(down_done, nth(tb, E, e))
                    if e:
                        dve.wait_ge(mixed, nth(tb, E * TT, TT * e - 1))
                    else:
                        dve.wait_ge(route, nth(tb, N_ROUTE, N_ROUTE - 1))
                        if not is_first(tb):
                            dve.wait_ge(stored, nth(tb - 1, 16, 15))
                    for tt in range(TT):
                        dve.scalar_tensor_tensor(out=mix[:, tt, :], in0=m_bank[e % 2][:, tt * C:tt * C + C],
                                                 scalar=comb[:, tt, e:e + 1], in1=(mix if e else h_sb)[:, tt, :],
                                                 op0=ALU.mult, op1=ALU.add).then_inc(mixed, 1)

                def spread(s, at, n, slot):
                    part = 4 * (s - at) + slot
                    return (part,) if at <= s and part < n else ()

                def slot_work(b, s, slot):
                    if not is_last(b):
                        if s == LN_P_AT and slot == 0:
                            dve.wait_ge(xp_in, nth(b + 1, 16, 15))
                        for part in spread(s, LN_P_AT, LN_STAGES, slot):
                            layernorm_stage(dve, part, b + 1, xp, xp, ln_p, ln_p_done, dve_passed)
                    for tb, ts in tails(b, s):
                        if ts == LN_H_AT and slot == 0:
                            dve.wait_ge(h_done, nth(tb, 1, 0))
                        for part in spread(ts, LN_H_AT, LN_STAGES, slot):
                            layernorm_stage(dve, part, tb, h_sb, xn, ln_h, ln_h_done, dve_passed)
                        for n in ROUTE.get(ts, ((),) * 4)[slot]:
                            route_step(tb, n)
                        if ts == LN_O_AT and slot == 0:
                            dve.wait_ge(bias_done, nth(tb, 2 * E, 2 * E - 1))
                            dve.wait_ge(mixed, nth(tb, E * TT, E * TT - 1))
                            dve.tensor_tensor(mix[:, :, :], mix[:, :, :], zp[:, :, :], ALU.add).then_inc(sum_done, 1)
                            dve.wait_ge(sum_done, nth(tb, 1, 0))
                        for part in spread(ts, LN_O_AT, LN_STAGES, slot):
                            layernorm_stage(dve, part, tb, mix, mix, ln_o, ln_o_done, dve_passed)

                def body(b):
                    if is_first(b):
                        dve.wait_ge(xp_in, 16)
                        for part in range(LN_STAGES):
                            layernorm_stage(dve, part, 0, xp, xp, ln_p, ln_p_done, dve_passed)
                        split_ht(0)
                    for s in steps(b):
                        if s == 13 and not is_last(b):
                            split_ht(b + 1)
                        if live(b, s):
                            i = s % NPB
                            wait_nth(dve, pt_done, b, H, s - NPB)
                            dve.wait_ge(scores_done, nth(b, H, s))
                            hold(dve, dve_passed)
                            for j, seg in enumerate(SEGS):
                                dve.tensor_tensor_reduce(probs[i][:, seg], s_bank[:, seg], mask[:, seg], 1.0, MASKED,
                                                         ALU.add, ALU.max, row_max[:, i, j:j + 1]).then_inc(masked, 1)
                            dve.wait_ge(masked, nth(b, 2 * H, 2 * s + 1))
                            dve.tensor_scalar(neg_max[:, i, :], row_max[:, i, :], -SCALE, None, ALU.mult)\
                               .then_inc(neg_done, 1)
                        slot_work(b, s, 0)
                        if live(b, s - LAG_PV):
                            k = s - LAG_PV
                            dve.wait_ge(ot_hi_done, nth(b, H, k))
                            dve.scalar_tensor_tensor(out=ot_lo[k % 2][:, :], in0=o_bank[:, 0:T],
                                                     scalar=col("bv", k % H), in1=ot_hi[k % 2][:, :].bitcast(F32),
                                                     op0=ALU.add, op1=ALU.subtract).then_inc(ot_lo_done, 1)
                        if live(b, s):
                            dve.wait_ge(exp_done, nth(b, H, s))
                            dve.reciprocal(row_inv[:, s % NPB, :], row_sum[:, s % NPB, :]).then_inc(inv_done, 1)
                        for tb, ts in tails(b, s):
                            if ts == LAG_O - 1:
                                dve.wait_ge(o_proj, nth(tb, H, H - 1))
                                dve.wait_ge(hb_done, nth(tb, 1, 0))
                                dve.tensor_tensor(flat(h_sb[:, :, :]), y_bank[:, :], flat(h_sb[:, :, :]), ALU.add)\
                                   .then_inc(h_done, 1)
                        slot_work(b, s, 1)
                        for tb, ts in tails(b, s):
                            if ts in (14, 18):
                                for e in (0, 1) if ts == 14 else (2, 3):
                                    mix_expert(tb, e)
                        slot_work(b, s, 2)
                        if live(b, s + 2):
                            k = s + 2
                            wait_swap(dve, b, k)
                            dve.tensor_tensor(qk_swap[k % 2][:, :, :], qk_swap[k % 2][:, :, :], sin, ALU.mult)\
                               .then_inc(rope_done, 1)
                            dve.tensor_tensor(qk[k % 2][:, :, :], qk[k % 2][:, :, :], cos, ALU.mult)\
                               .then_inc(rope_done, 1)
                        slot_work(b, s, 3)
                        c = s + 2
                        if is_first(b) and 0 <= c < N_WO:
                            dve.wait_ge(wo_hi_done, c + 1)
                            at = slice(c * WO_CH, (c + 1) * WO_CH)
                            dve.tensor_tensor(wo_lo[:, :, :].rearrange("p h c -> p (h c)")[:, at],
                                              flat(units[c % 2][:, :, :]),
                                              wo_hi[:, :, :].rearrange("p h c -> p (h c)")[:, at].bitcast(F32),
                                              ALU.subtract).then_inc(wo_lo_done, 1)
                walk(dve, body)

            @block.tensor
            def _(pe):
                def transpose_tokens(src, dst):
                    for k in range(KC):
                        for tt in range(TT):
                            ins = pe.transpose(dst[:, k * T + tt * P:k * T + tt * P + P], src[:, tt, k * P:k * P + P],
                                               ident)
                    return ins

                def prepare(nb):
                    pe.wait_ge(ln_p_done, nth(nb, LN_STEPS, LN_STEPS - 1))
                    if not is_first(nb):
                        if not (isinstance(nb, int) and nb == 1):
                            pe.wait_ge(h2t_done, nth(nb - 2, KC, KC - 1))
                        else:
                            pe.wait_ge(ht_done, nth(0, KC, KC - 1))
                    transpose_tokens(xp, m_bank[0]).then_inc(xpt_done, 1)

                def project_qk(b, k):
                    if k % H == 0:
                        pe.wait_ge(ht_parts, nth(b, 2, k // H * 2 + 1))
                    wait_nth(pe, qk_done, b, 2 * H, 2 * (k - 1) + 1)
                    for j in range(2):
                        for c in range(KC):
                            at = (j * KC + c) * H * HSB + (k % H) * HSB
                            ins = three_passes(pe, qk_bank[:, j * T:j * T + T], w_qkv_hi[:, at:at + HSB],
                                               w_qkv_lo[:, at:at + HSB], ht_hi[:, c, :], ht_lo[:, c, :],
                                               start=(c == 0), stop=(c == KC - 1))
                    ins.then_inc(qk_proj, 1)

                def project_v(b, k):
                    wait_nth(pe, v_done, b, VPAIRS, k // 2 - 1)
                    for tt in range(TT):
                        tok = slice(tt * P, tt * P + P)
                        for c in range(KC):
                            at = (2 * KC + c) * H * HSB + (k % H) * HSB
                            ins = three_passes(pe, v_bank[:, tt * 2 * HSB:(tt + 1) * 2 * HSB], ht_hi[:, c, tok],
                                               ht_lo[:, c, tok], w_qkv_hi[:, at:at + 2 * HSB],
                                               w_qkv_lo[:, at:at + 2 * HSB], start=(c == 0), stop=(c == KC - 1))
                    ins.then_inc(v_proj, 1)

                def expert(tb, e, down):
                    bank_, done = m_bank[e % 2], down_done if down else up_done
                    if down:
                        pe.wait_ge(units_done, nth(tb, E * KC, KC * e + KC - 1))
                    elif e >= 2:
                        pe.wait_ge(mixed, nth(tb, E * TT, TT * (e - 1) - 1))
                    for i in range(2):
                        for c in range(KC):
                            if down:
                                args = units[e % 2][:, c, i * P:i * P + P], w_down[:, e, c, :]
                            else:
                                args = w_up[:, e, c, i * P:i * P + P], h2t[:, c, :]
                            ins = pe.matmul(bank_[:, i * T:i * T + T], *args, start=(c == 0), stop=(c == KC - 1),
                                            skip_group_check=True)
                    ins.then_inc(done, 1)

                def body(b):
                    if is_first(b):
                        prepare(0)
                    for s in steps(b):
                        if live(b, s):
                            pe.wait_ge(rot_done, nth(b, H, s))
                            wait_nth(pe, masked, b, 2 * H, 2 * (s - 1) + 1)
                            rot = qk_rot[s % 2]
                            for tt, seg in enumerate(SEGS):
                                ins = pe.matmul(s_bank[:, seg], rot[:, 0, tt * P:tt * P + P],
                                                rot[:, 1, 0:seg.stop - seg.start], start=True, stop=True)
                            ins.then_inc(scores_done, 1)
                        if live(b, s - LAG_O):
                            k = s - LAG_O
                            head = k % H
                            pe.wait_ge(ot_lo_done, nth(b, H, k))
                            if is_first(b) and 0 <= k < H:
                                pe.wait_ge(wo_lo_done, k * C // WO_CH + 1)
                            if head == 0 and not is_first(b):
                                pe.wait_ge(h_done, nth(b - 1, 1, 0))
                            for tt in range(TT):
                                tok = slice(tt * P, tt * P + P)
                                ins = three_passes(pe, y_bank[:, tt * C:tt * C + C], ot_hi[k % 2][:, tok],
                                                   ot_lo[k % 2][:, tok], wo_hi[:, head, :], wo_lo[:, head, :],
                                                   start=(head == 0 and tt == 0), stop=(head == H - 1))
                            ins.then_inc(o_proj, 1)
                        if live(b, s - LAG_PV):
                            k = s - LAG_PV
                            pe.wait_ge(pt_copied, nth(b, H, k))
                            if k % 2 == 0:
                                pe.wait_ge(v_done, nth(b, VPAIRS, k // 2))
                            wait_nth(pe, ot_lo_done, b, H, k - 1)
                            v, pt = v_sb[k // 2 % 2], pt_sb[k % 2]
                            pe.matmul(o_bank[:, 0:T], v[:, 0, k % 2, :], pt[:, 0:T], start=True, stop=False,
                                      skip_group_check=True)
                            pe.matmul(o_bank[:, P:T], v[:, 1, k % 2, :], pt[:, T:3 * P], start=False, stop=True,
                                      skip_group_check=True).then_inc(pv_done, 1)
                        for tb, ts in tails(b, s):
                            if ts in (13, 17):
                                for e in (0, 1) if ts == 13 else (2, 3):
                                    expert(tb, e, down=True)
                        if live(b, s + LEAD):
                            project_qk(b, s + LEAD)
                        if live(b, s - LAG_T):
                            k = s - LAG_T
                            pe.wait_ge(probs_done, nth(b, H, k))
                            wait_nth(pe, pt_copied, b, H, k - 1)
                            for c in range(3):
                                ins = pe.transpose(t_bank[:, c * P:c * P + P], probs[k % NPB][:, c * P:c * P + P], ident)
                            ins.then_inc(pt_done, 1)
                        if s % 2 == 0 and live(b, s + 2):
                            project_v(b, s + 2)
                        if s == 8 and not is_last(b):
                            prepare(b + 1)
                        for tb, ts in tails(b, s):
                            if ts == 7:
                                pe.wait_ge(ln_h_done, nth(tb, LN_STEPS, LN_STEPS - 1))
                                if is_first(tb):
                                    pe.wait_ge(ht_done, nth(tb + 1, KC, KC - 1))
                                else:
                                    pe.wait_ge(mixed, nth(tb - 1, E * TT, E * TT - 1))
                                transpose_tokens(xn, m_bank[0]).then_inc(h2t_psum, 1)
                            if ts == 8:
                                pe.wait_ge(h2t_done, nth(tb, KC, KC - 1))
                                for tt in range(TT):
                                    for c in range(KC):
                                        a = COLS["w_gate"][0] + c * E
                                        ins = pe.matmul(m_bank[1][:, tt * E:tt * E + E], h2t[:, c, tt * P:tt * P + P],
                                                        cols[:, a:a + E], start=(c == 0), stop=(c == KC - 1),
                                                        skip_group_check=True)
                                ins.then_inc(logits_psum, 1)
                            if ts in (11, 15):
                                if ts == 11:
                                    pe.wait_ge(moe_in, 32)
                                    pe.wait_ge(route, nth(tb, N_ROUTE, R_SHIFTED))
                                    if not (isinstance(tb, int) and tb >= NB - 2):
                                        pe.wait_ge(ht_done, nth(tb + 2, KC, KC - 1))
                                for e in (0, 1) if ts == 11 else (2, 3):
                                    expert(tb, e, down=False)
                walk(pe, body)


def build(nc, x, w_attn_a, w_out_a, consts_dram, w_qkv, w_out_b, w_moe, cols_dram, rows_dram, out):
    x1 = nc.dram_tensor("x1", (NB, T, C), F32, kind="Internal").ap()
    with ExitStack() as ctx:
        w_hi = ctx.enter_context(nc.sbuf_tensor("w_hi", [P, QKVW], F32R))
        w_lo = ctx.enter_context(nc.sbuf_tensor("w_lo", [P, QKVW], F32R))
        consts = ctx.enter_context(nc.sbuf_tensor("consts", [P, NSHARED], F32))
        layer_a(nc, x, w_attn_a, w_out_a, consts_dram, w_qkv, x1, w_hi, w_lo, consts)
        layer_b(nc, x1, w_hi, w_lo, w_out_b, w_moe, cols_dram, rows_dram, out, consts)


def make_consts():
    f32 = np.float32
    i, j = np.arange(T)[:, None], np.arange(T)[None, :]

    def mask_rows(allowed):
        m = np.where(allowed, 0.0, MASKED)
        return np.concatenate([m[:P, :P], m[P:, :]], axis=1)

    causal = j <= i
    window = causal & ((j >= i - (WINDOW - 1)) | (j < SINK))
    inv_freq = (1.0 / f32(ROPE_THETA) ** (np.arange(0, HSB, 2, dtype=f32) / f32(HSB))).astype(f32)
    freqs = np.arange(T, dtype=f32)[:, None] * inv_freq[None, :]
    cos, sin = (np.concatenate([f(freqs), f(freqs)], axis=1).T for f in (np.cos, np.sin))
    sin = np.concatenate([-sin[:HSB // 2], sin[HSB // 2:]], axis=0)
    p = np.arange(P)[:, None]
    values = {
        "ident": np.eye(P),
        "mask_a": mask_rows(window), "mask_b": mask_rows(causal),
        "cos": cos, "sin": sin,
        "qneg": np.where(p % (2 * HSA) >= HSA, -1.0, 0.0),
        "kneg": np.where(p % (4 * HSA) >= 2 * HSA, -1.0, 0.0),
        "before": np.broadcast_to(np.tril(np.ones((E, E)), -1).reshape(1, E * E), (P, E * E)),
    }
    return np.ascontiguousarray(np.concatenate([values[name] for name in CONSTS], axis=1), dtype=f32)


def kernel(**inputs):
    import concourse.bacc as _bacc
    from concourse.bass_utils import run_bass_kernel_spmd as _run

    a = {name[len("L0_attn_"):]: np.asarray(v) for name, v in inputs.items() if name.startswith("L0_attn_")}
    f = {name[len("L0_ffn_"):]: np.asarray(v) for name, v in inputs.items() if name.startswith("L0_ffn_")}

    def to_partitions(v, inner):
        return np.moveaxis(v.reshape(-1, P, inner), 1, 0).reshape(P, -1)

    params = {name: to_partitions(f[name].reshape(-1, 1), 1) for name in COLS if name != "w_gate"}
    params["w_gate"] = to_partitions(f["w_gate"], E)
    arrays = {
        "x": a["x"],
        "w_attn_a": np.concatenate([a["Wv"].T, a["Wk"].T, a["Wq"].T], axis=1),
        "w_out_a": a["Wo"].T,
        "consts": make_consts(),
        "w_qkv": np.concatenate([to_partitions(f[name], H * HSB) for name in ("wq", "wk", "wv")], axis=1),
        "w_out_b": to_partitions(f["wo"], C),
        "w_moe": np.concatenate([to_partitions(f[name], C) for name in ("we1", "we2")], axis=1),
        "cols": np.concatenate([params[name] for name in COLS], axis=1),
        "rows": np.broadcast_to(np.concatenate([f["bo"], f["be2"].reshape(-1)])[None, :], (P, NROWS)),
    }
    arrays = {name + "_dram": np.ascontiguousarray(v) for name, v in arrays.items()}

    nc = _bacc.Bacc("TRN2", target_bir_lowering=False, num_devices=1)
    args = [nc.dram_tensor(name, v.shape, F32, kind="ExternalInput").ap() for name, v in arrays.items()]
    out = nc.dram_tensor("out_dram", (NB, T, C), F32, kind="ExternalOutput").ap()
    build(nc, *args, out)
    r = _run(nc, [arrays], core_ids=[0])
    return r.results[0]["out_dram"]
```

```python
from contextlib import ExitStack

import numpy as np

import concourse.bass as bass
from concourse import mybir

F32 = mybir.dt.float32
F32R = mybir.dt.float32r
I32 = mybir.dt.int32
ALU = mybir.AluOpType
ACT = mybir.ActivationFunctionType
AX = mybir.AxisListType

P = 128
NB, T, C = 8, 256, 256
TT, KC = T // P, C // P
H = 16
HSA, KVA = 16, 4
WINDOW, SINK = 128, 4
HSB = 128
E = 4
EPS = 1e-5
ROPE_THETA = 10000.0
MASKED = -1.0e30
REP = 2
HPT = P // HSA
RSQRT_GUESS = 0x5F3759DF
WCH = 384
QKVW = 3 * KC * H * HSB

CONSTS = {}
_at = 0
for _name, _n in (("ident", P), ("mask_b", 3 * P), ("cos", T), ("sin", T), ("before", E * E),
                  ("mask_a", 3 * P)):
    CONSTS[_name] = (_at, _at + _n)
    _at += _n
NCONST = _at
COLS = {}
_at = 0
for _name, _n in (("bq", H), ("bk", H), ("bv", H), ("ln1_w", KC), ("ln1_b", KC), ("ln2_w", KC),
                  ("ln2_b", KC), ("be1", E * KC), ("w_gate", KC * E)):
    COLS[_name] = (_at, _at + _n)
    _at += _n
NCOLS = _at
ROWS = {"bo": (0, C), "be2": (C, C + E * C)}
NROWS = C + E * C
NSHARED = CONSTS["before"][1]


def const(consts, name):
    a, b = CONSTS[name]
    return consts[:, a:b]


def walk_batches(eng, body):
    body(0)
    with eng.Fori(1, NB - 1) as b:
        body(b)
    body(NB - 1)


def is_first(b):
    return isinstance(b, int) and b == 0


def is_last(b):
    return isinstance(b, int) and b == NB - 1


def live(b, k):
    return not (is_first(b) and k < 0) and not (is_last(b) and k >= H)


def nth(b, per, k):
    return b * per + (k + 1)


def wait_nth(eng, sem, b, per, k):
    if not (isinstance(b, int) and b * per + k < 0):
        eng.wait_ge(sem, nth(b, per, k))


def x1_stored(n):
    return 16 * n + 16


def hold(eng, passed):
    eng.sem_inc(passed, 1)


def flat(ap):
    return ap.rearrange("p a b -> p (a b)")


LN_COUNTS = (2, 2, 1, 1) + (1,) * 9 + (2,)
LN_STAGES, LN_STEPS = len(LN_COUNTS), sum(LN_COUNTS)


def layernorm_stage(dve, stage, b, src, dst, ln, done, dve_passed):
    stats, mv, work = ln
    var, y, t = (work[:, i, :] for i in range(3))
    if stage > 0:
        dve.wait_ge(done, nth(b, LN_STEPS, sum(LN_COUNTS[:stage]) - 1))
    if stage == 0:
        for tt in range(TT):
            dve.bn_stats(stats[:, tt, :], src[:, tt, :]).then_inc(done, 1)
    elif stage == 1:
        hold(dve, dve_passed)
        for tt in range(TT):
            dve.bn_aggr(mv[:, tt, :], stats[:, tt, :]).then_inc(done, 1)
    elif stage == 2:
        dve.tensor_scalar(var, mv[:, :, 1], EPS, None, ALU.add).then_inc(done, 1)
    elif stage == 3:
        dve.tensor_scalar(y.bitcast(I32), var.bitcast(I32), -0.5, float(RSQRT_GUESS), ALU.mult, ALU.add)\
           .then_inc(done, 1)
    elif stage == LN_STAGES - 1:
        for tt in range(TT):
            dve.tensor_scalar(dst[:, tt, :], src[:, tt, :], mv[:, tt, 0:1], y[:, tt:tt + 1],
                              ALU.subtract, ALU.mult).then_inc(done, 1)
    elif stage % 3 == 1:
        dve.tensor_tensor(t, y, y, ALU.mult).then_inc(done, 1)
    elif stage % 3 == 2:
        dve.scalar_tensor_tensor(out=t, in0=t, scalar=-0.5, in1=var, op0=ALU.mult, op1=ALU.mult).then_inc(done, 1)
    else:
        dve.scalar_tensor_tensor(out=y, in0=t, scalar=1.5, in1=y, op0=ALU.add, op1=ALU.mult).then_inc(done, 1)


def three_passes(pe, out, lhs_hi, lhs_lo, rhs_hi, rhs_lo, start, stop):
    pe.matmul(out, lhs_lo, rhs_hi, start=start, stop=False, skip_group_check=True)
    pe.matmul(out, lhs_hi, rhs_lo, start=False, stop=False, skip_group_check=True)
    return pe.matmul(out, lhs_hi, rhs_hi, start=False, stop=stop, skip_group_check=True)


def transpose_tokens(pe, src, dst, ident):
    for k in range(KC):
        for tt in range(TT):
            ins = pe.transpose(dst[:, k * T + tt * P:k * T + tt * P + P], src[:, tt, k * P:k * P + P], ident)
    return ins


def split_parts(dve, nb, ht, hi, lo, shared):
    dve.wait_ge(shared.ht_done, nth(nb, KC, KC - 1))
    dve.tensor_copy(hi[:, :, :], ht[:, :, :]).then_inc(shared.ht_parts, 1)
    dve.wait_ge(shared.ht_parts, nth(nb, 2, 0))
    dve.tensor_tensor(lo[:, :, :], ht[:, :, :], hi[:, :, :].bitcast(F32), ALU.subtract).then_inc(shared.ht_parts, 1)


def column(cols, name, i):
    a = COLS[name][0] + i
    return cols[:, a:a + 1]


def layer_a(nc, x, w_attn, w_out, consts_dram, w_qkv, cols_dram, x1, shared):
    w_hi, w_lo, consts, cols = shared.w_hi, shared.w_lo, shared.consts, shared.cols
    xt_hi, xt_lo, res, x1_out = shared.xt_hi, shared.xt_lo, shared.res, shared.x1_out
    VC = KVA * HSA
    NQ = HPT // 2
    SCALE = HSA ** -0.5
    LAG_T, LAG_COPY, LAG_PV = 3, 4, 6
    TAIL_STEPS = 16
    NPT = 4
    XT_AT, KV_AT, Q_AT, VT_AT = 3, 5, 6, 8
    B_LN_AT, B_XT_AT, B_AFFINE_AT, B_PARTS_AT = 3, 12, 13, 14
    LN_AT = LAG_PV + 3
    SPLIT = (0, 2, 10, 12)
    NCH = len(SPLIT)
    NPB = 4

    with ExitStack() as ctx:
        def sb(name, shape, dt=F32):
            return ctx.enter_context(nc.sbuf_tensor("a_" + name, shape, dt))

        def bank(name):
            return ctx.enter_context(nc.psum_tensor("a_" + name, [P, 512], F32))

        def sem(name):
            return ctx.enter_context(nc.semaphore("a_" + name))

        w_raw = sb("w_raw", [P, KC, 2 * VC + H * HSA])
        mask = sb("mask", [P, NCONST - NSHARED])
        wo_raw = sb("wo_raw", [P, KC, C])
        wa_hi, wa_lo = (sb(n, [P, KC, 2 * VC + H * HSA], F32R) for n in ("wa_hi", "wa_lo"))
        wo_hi, wo_lo = (sb(n, [P, KC, C], F32R) for n in ("wo_hi", "wo_lo"))
        xs = sb("xs", [P, TT, C])
        xr = sb("xr", [P, TT, C])
        q_parts = sb("q_parts", [P, TT, 2, T], F32R)
        k_parts = sb("k_parts", [P, 2, T], F32R)
        vt = sb("vt", [VC, T])
        q_stack = sb("q_stack", [P, H // 2, T], F32R)
        k_stack = [sb(f"k_stack{i}", [P, KVA, T], F32R) for i in range(2)]
        v_sb = sb("v_sb", [P, TT, KVA, HSA])
        ZW = 2 * P - HSA
        v_pad = sb("v_pad", [P, TT, KVA, ZW])
        probs = [sb(f"probs{i}", [P, 3 * P]) for i in range(NPB)]
        neg_max = sb("neg_max", [P, NPB, 2])
        row_max = sb("row_max", [P, NPB, 2])
        row_sum = sb("row_sum", [P, NPB, 2])
        row_inv = sb("row_inv", [P, NPB, 2])
        pt_sb = [sb(f"pt_sb{i}", [P, 3 * P]) for i in range(NPT)]
        yt_hi, yt_lo = (sb(n, [P, KC, T], F32R) for n in ("yt_hi", "yt_lo"))
        ln = sb("stats", [P, TT, 6]), sb("mv", [P, TT, 2]), sb("work", [P, 3, TT])
        stage = [sb(f"stage{i}", [P, WCH]) for i in range(NCH)]

        s_bank = [bank(f"scores{i}") for i in range(2)]
        t_bank = [bank(f"p_t{i}") for i in range(2)]
        o_bank = [bank(f"o_t{i}") for i in range(2)]
        p_bank = [bank(f"proj{i}") for i in range(2)]

        consts_in, mask_in, w_in = sem("consts_in"), sem("mask_in"), sem("w_in")
        x_in, xr_in = sem("x_in"), sem("xr_in")
        stage_in = [sem(f"stage_in{i}") for i in range(NCH)]
        w_split, w_split_hi, zeroed, wo_in = sem("w_split"), sem("w_split_hi"), sem("zeroed"), sem("wo_in")
        xt_done, xt_hi_done, xt_lo_done = sem("xt_done"), sem("xt_hi_done"), sem("xt_lo_done")
        kv_proj, q_proj, vt_done, v_psum = sem("kv_proj"), sem("q_proj"), sem("vt_done"), sem("v_psum")
        k_hi_done, k_lo_done, q_hi_done, q_lo_done = (
            sem(n) for n in ("k_hi_done", "k_lo_done", "q_hi_done", "q_lo_done"))
        k_out, q_out = sem("k_out"), sem("q_out")
        k_in, q_in = ([sem(f"{n}{i}") for i in range(2)] for n in ("k_in", "q_in"))
        v_done, v_pad_done = sem("v_done"), sem("v_pad_done")
        scores_done, masked, neg_done = sem("scores_done"), sem("masked"), sem("neg_done")
        exp_done, inv_done, probs_done = sem("exp_done"), sem("inv_done"), sem("probs_done")
        pt_done, pt_sb_act, pt_sb_dve = sem("pt_done"), sem("pt_sb_act"), sem("pt_sb_dve")
        pv_done, yt_hi_done, yt_lo_done = sem("pv_done"), sem("yt_hi_done"), sem("yt_lo_done")
        y_done, res_done, ln_done, cols_in = sem("y_done"), sem("res_done"), sem("ln_done"), sem("cols_in")
        dve_passed, pool_passed, pe_passed, sp_passed = (sem(n + "_passed") for n in ("dve", "pool", "pe", "sp"))
        stage_hi, stage_lo = sem("stage_hi"), sem("stage_lo")

        x_view = x.rearrange("b (t p) c -> b p t c", p=P)
        x1_view = x1.rearrange("b (t p) c -> b p t c", p=P)
        ident = const(consts, "ident")

        q_dram = nc.dram_tensor("q_scratch", (NB, TT, 2, HSA, 2, NQ * T), F32, kind="Internal").ap()
        k_dram = nc.dram_tensor("k_scratch", (NB, 2, REP, HSA, KVA * T), F32, kind="Internal").ap()
        q_write = q_dram.rearrange("b t l d h (q n) -> b (d h q) (t l) n", q=NQ)
        k_write = k_dram.rearrange("b l r d (g n) -> b r (d g) l n", g=KVA)
        q_read = q_dram.rearrange("b t l d h n -> b t h (l d) n")
        k_read = k_dram.rearrange("b l r d n -> b (l r d) n")
        QS, KS = 2 * REP, 2

        def stack_q(sp, nb, t):
            for h in range(2):
                for copy in range(REP):
                    row = (h * REP + copy) * 2 * HSA
                    sp.dma_start(q_stack[row:row + 2 * HSA, t * NQ:t * NQ + NQ, :].bitcast(F32)
                                 .rearrange("p q n -> p (q n)"), q_read[nb, t, h]).then_inc(q_in[t], 16)

        def stack_k(sp, nb, t):
            groups = KVA // 2
            for h in range(2):
                row = h * 2 * REP * HSA
                sp.dma_start(k_stack[h][row:row + 2 * REP * HSA, t * groups:(t + 1) * groups, :].bitcast(F32)
                             .rearrange("p g n -> p (g n)"),
                             k_read[nb][:, t * groups * T:(t + 1) * groups * T]).then_inc(k_in[t], 16)

        def steps(b):
            return range(H + TAIL_STEPS if is_last(b) else H)

        def tail_of(b, s):
            if s >= H:
                return b, s - H
            return (None, None) if is_first(b) else (b - 1, s)

        with nc.Block() as block:
            @block.sync
            def _(sp):
                sp.sem_inc(x1_out, 16)
                sp.dma_start(w_raw[:, :, :], w_attn.rearrange("(k p) n -> p k n", p=P)).then_inc(w_in, 16)
                sp.dma_start(xs[:, :, :], x_view[0]).then_inc(x_in, 16)
                sp.dma_start(consts[:, :], consts_dram[:, 0:NSHARED]).then_inc(consts_in, 16)
                sp.dma_start(mask[:, :], consts_dram[:, NSHARED:NCONST]).then_inc(mask_in, 16)
                sp.dma_start(cols[:, :], cols_dram).then_inc(cols_in, 16)
                sp.dma_start(wo_raw[:, :, :], w_out.rearrange("(k p) n -> p k n", p=P)).then_inc(wo_in, 16)

                def store_x1(tb):
                    sp.wait_ge(ln_done, nth(tb, LN_STEPS, LN_STEPS - 1))
                    sp.dma_start(x1_view[tb], res[:, :, :]).then_inc(x1_out, 16)

                def write_k(nb):
                    sp.wait_ge(k_lo_done, nth(nb, 1, 0))
                    for copy in range(REP):
                        sp.dma_start(k_write[nb, copy], k_parts[VC:2 * VC, :, :].bitcast(F32)).then_inc(k_out, 16)

                def write_q(nb):
                    sp.wait_ge(q_lo_done, nth(nb, 1, 0))
                    sp.dma_start(q_write[nb], q_parts[:, :, :, :].bitcast(F32).rearrange("p t l n -> p (t l) n"))\
                      .then_inc(q_out, 16)

                def read_stacks(nb, t):
                    sp.wait_ge(k_out, nth(nb, 16 * REP, 16 * REP - 1))
                    sp.wait_ge(q_out, nth(nb, 16, 15))
                    hold(sp, sp_passed)
                    if is_first(nb):
                        sp.wait_ge(zeroed, 3)
                    else:
                        sp.wait_ge(scores_done, nth(nb - 1, H, HPT * t + HPT - 1))
                    stack_k(sp, nb, t)
                    stack_q(sp, nb, t)

                def load_chunk(b, i):
                    if not is_first(b):
                        sp.wait_ge(stage_lo, nth(b - 1, NCH, i))
                    sp.dma_start(stage[i][:, :], w_qkv[:, bass.ds(b * (NCH * WCH) + i * WCH, WCH)])\
                      .then_inc(stage_in[i], 16)

                def body(b):
                    if not is_last(b):
                        sp.wait_ge(xt_done, nth(b, 1, 0))
                        sp.dma_start(xs[:, :, :], x_view[b + 1]).then_inc(x_in, 16)
                    else:
                        sp.wait_ge(xt_done, NB)
                        sp.wait_ge(x1_out, x1_stored(1))
                        sp.dma_start(xs[:, :, :], x1_view[0]).then_inc(shared.xp_in, 16)
                    if is_first(b):
                        write_k(0)
                        write_q(0)
                        read_stacks(0, 0)
                    read_stacks(b, 1)
                    if is_first(b):
                        for i in range(NCH):
                            load_chunk(0, i)
                    if not is_last(b):
                        write_k(b + 1)
                        write_q(b + 1)
                        read_stacks(b + 1, 0)
                    if not is_first(b):
                        sp.wait_ge(res_done, nth(b - 1, 1, 0))
                        hold(sp, sp_passed)
                    sp.dma_start(xr[:, :, :], x_view[b]).then_inc(xr_in, 16)
                    if not is_last(b):
                        for i in range(NCH):
                            load_chunk(b + 1, i)
                    if not is_first(b):
                        store_x1(b - 1)
                walk_batches(sp, body)
                store_x1(NB - 1)

            @block.gpsimd
            def _(pool):
                for i in range(2):
                    pool.memset(k_stack[i][:, :, :].bitcast(F32), 0.0).then_inc(zeroed, 1)
                pool.memset(v_pad[:, :, :, :], 0.0).then_inc(zeroed, 1)

                def v_pad_copy(nb, half):
                    pool.wait_ge(v_done, nth(nb, 1, 0))
                    if is_first(nb):
                        pool.wait_ge(zeroed, 3)
                    else:
                        pool.wait_ge(pv_done, nth(nb - 1, H, 8 * half + 7))
                    hold(pool, pool_passed)
                    for g in (2 * half, 2 * half + 1):
                        pool.tensor_copy(v_pad[:, :, g, P - HSA:P], v_sb[:, :, g, :]).then_inc(v_pad_done, 1)

                def body(b):
                    if is_first(b):
                        v_pad_copy(0, 0)
                    for s in steps(b):
                        if live(b, s - 1):
                            pool.wait_ge(inv_done, nth(b, H, s - 1))
                            i = (s - 1) % NPB
                            for j, seg in enumerate((slice(0, P), slice(P, 3 * P))):
                                n = seg.stop - seg.start
                                ins = pool.tensor_tensor(probs[i][:, seg], probs[i][:, seg],
                                                         row_inv[:, i, j:j + 1].broadcast_to([P, n]), ALU.mult)
                            ins.then_inc(probs_done, 1)
                        if s - 1 in SPLIT:
                            i = SPLIT.index(s - 1)
                            pool.wait_ge(stage_hi, nth(b, NCH, i))
                            at = bass.ds(b * (NCH * WCH) + i * WCH, WCH)
                            pool.tensor_tensor(w_lo[:, at], stage[i][:, :], w_hi[:, at].bitcast(F32),
                                              ALU.subtract).then_inc(stage_lo, 1)
                        if s == 7:
                            v_pad_copy(b, 1)
                        if s == 15 and not is_last(b):
                            v_pad_copy(b + 1, 0)
                walk_batches(pool, body)

            @block.scalar
            def _(act):
                act.wait_ge(w_in, 16)
                for k in range(KC):
                    act.activation(wa_hi[:, k, :], w_raw[:, k, :], ACT.Copy).then_inc(w_split_hi, 1)

                def xt_high(nb):
                    act.wait_ge(xt_done, nth(nb, 1, 0))
                    if not is_first(nb):
                        act.wait_ge(q_proj, nth(nb - 1, 1, 0))
                    act.activation(flat(xt_hi[:, :, :]), p_bank[1][:, :], ACT.Copy).then_inc(xt_hi_done, 1)

                def kv_high(nb):
                    act.wait_ge(kv_proj, nth(nb, 1, 0))
                    if not is_first(nb):
                        act.wait_ge(v_psum, nth(nb - 1, 1, 0))
                        act.wait_ge(k_out, nth(nb - 1, 16 * REP, 16 * REP - 1))
                    act.activation(vt[:, :], p_bank[0][0:VC, 0:T], ACT.Copy).then_inc(vt_done, 1)
                    act.activation(k_parts[VC:2 * VC, 0, :], p_bank[0][VC:2 * VC, 0:T], ACT.Copy).then_inc(k_hi_done, 1)

                def q_high(nb):
                    act.wait_ge(q_proj, nth(nb, 1, 0))
                    if not is_first(nb):
                        act.wait_ge(q_out, nth(nb - 1, 16, 15))
                    act.activation(q_parts[:, :, 0, :], p_bank[1][:, :].rearrange("p (t n) -> p t n", t=TT),
                                   ACT.Copy).then_inc(q_hi_done, 1)

                def v_copy(nb):
                    act.wait_ge(v_psum, nth(nb, 1, 0))
                    if not is_first(nb):
                        act.wait_ge(v_pad_done, nth(nb - 1, KVA, KVA - 1))
                    act.activation(v_sb[:, :, :, :].rearrange("p t g d -> p (t g d)"), p_bank[0][:, 0:TT * VC],
                                   ACT.Copy).then_inc(v_done, 1)

                def yt_high(tb, t):
                    act.wait_ge(pv_done, nth(tb, H, HPT * t + HPT - 1))
                    act.activation(yt_hi[:, t, :], o_bank[t][:, 0:T], ACT.Copy).then_inc(yt_hi_done, 1)

                def body(b):
                    if is_first(b):
                        xt_high(0)
                        kv_high(0)
                        q_high(0)
                        v_copy(0)
                        act.wait_ge(wo_in, 16)
                        act.activation(flat(wo_hi[:, :, :]), flat(wo_raw[:, :, :]), ACT.Copy).then_inc(w_split_hi, 1)
                    for s in steps(b):
                        if s == XT_AT + 1 and not is_last(b):
                            xt_high(b + 1)
                        if live(b, s - LAG_COPY) and (s - LAG_COPY) % 2 == 0:
                            k = s - LAG_COPY
                            act.wait_ge(pt_done, nth(b, H, k))
                            wait_nth(act, pv_done, b, H, k - NPT)
                            act.activation(pt_sb[k % NPT][:, :], t_bank[k % 2][:, 0:3 * P], ACT.Copy)\
                               .then_inc(pt_sb_act, 1)
                        if not is_last(b):
                            if s == KV_AT + 1:
                                kv_high(b + 1)
                            if s == Q_AT + 1:
                                q_high(b + 1)
                            if s == VT_AT + 1:
                                v_copy(b + 1)
                        if live(b, s):
                            i = s % NPB
                            act.wait_ge(neg_done, nth(b, H, s))
                            for j, seg in enumerate((slice(0, P), slice(P, 3 * P))):
                                ins = act.activation(probs[i][:, seg], probs[i][:, seg], ACT.Exp,
                                                     bias=neg_max[:, i, j:j + 1], scale=SCALE,
                                                     accum_out=row_sum[:, i, j:j + 1])
                            ins.then_inc(exp_done, 1)
                        if s in SPLIT:
                            i = SPLIT.index(s)
                            act.wait_ge(stage_in[i], nth(b, 16, 15))
                            act.activation(w_hi[:, bass.ds(b * (NCH * WCH) + i * WCH, WCH)], stage[i][:, :],
                                           ACT.Copy).then_inc(stage_hi, 1)
                        tb, ts = tail_of(b, s)
                        if ts == LAG_PV:
                            yt_high(tb, 1)
                        if s == LAG_PV + HPT:
                            yt_high(b, 0)
                        if is_last(b) and s == B_AFFINE_AT:
                            act.wait_ge(cols_in, 16)
                            act.wait_ge(shared.xpt_done, 1)
                            for k in range(KC):
                                act.activation(xs[:, k, :], p_bank[1][:, k * T:k * T + T], ACT.Identity,
                                               bias=column(cols, "ln1_b", k), scale=column(cols, "ln1_w", k))\
                                   .then_inc(shared.ht_done, 1)
                walk_batches(act, body)

            @block.vector
            def _(dve):
                dve.wait_ge(w_in, 16)
                for k in range(KC):
                    dve.wait_ge(w_split_hi, k + 1)
                    dve.tensor_tensor(wa_lo[:, k, :], w_raw[:, k, :], wa_hi[:, k, :].bitcast(F32),
                                      ALU.subtract).then_inc(w_split, 1)

                def xt_low(nb):
                    dve.wait_ge(xt_hi_done, nth(nb, 1, 0))
                    dve.tensor_tensor(flat(xt_lo[:, :, :]), p_bank[1][:, :], flat(xt_hi[:, :, :].bitcast(F32)),
                                      ALU.subtract).then_inc(xt_lo_done, 1)

                def k_low(nb):
                    dve.wait_ge(k_hi_done, nth(nb, 1, 0))
                    dve.tensor_tensor(k_parts[VC:2 * VC, 1, :], p_bank[0][VC:2 * VC, 0:T],
                                      k_parts[VC:2 * VC, 0, :].bitcast(F32), ALU.subtract).then_inc(k_lo_done, 1)

                def q_low(nb):
                    dve.wait_ge(q_hi_done, nth(nb, 1, 0))
                    dve.tensor_tensor(q_parts[:, :, 1, :], p_bank[1][:, :].rearrange("p (t n) -> p t n", t=TT),
                                      q_parts[:, :, 0, :].bitcast(F32), ALU.subtract).then_inc(q_lo_done, 1)

                def yt_low(tb, t):
                    dve.wait_ge(yt_hi_done, nth(tb, 2, t))
                    dve.tensor_tensor(yt_lo[:, t, :], o_bank[t][:, 0:T], yt_hi[:, t, :].bitcast(F32),
                                      ALU.subtract).then_inc(yt_lo_done, 1)

                def layernorm_part(tb, ts, half):
                    if ts is not None and LN_AT <= ts < LN_AT + LN_STAGES // 2:
                        layernorm_stage(dve, 2 * (ts - LN_AT) + half, tb, res, res, ln, ln_done, dve_passed)

                def row_inverse(b, k):
                    dve.wait_ge(exp_done, nth(b, H, k))
                    dve.reciprocal(row_inv[:, k % NPB, :], row_sum[:, k % NPB, :]).then_inc(inv_done, 1)

                def body(b):
                    if is_first(b):
                        xt_low(0)
                        k_low(0)
                        q_low(0)
                        dve.wait_ge(mask_in, 16)
                        dve.wait_ge(w_split_hi, KC + 1)
                        dve.tensor_tensor(flat(wo_lo[:, :, :]), flat(wo_raw[:, :, :]), flat(wo_hi[:, :, :].bitcast(F32)),
                                          ALU.subtract).then_inc(w_split, 1)
                    for s in steps(b):
                        tb, ts = tail_of(b, s)
                        if ts == LN_AT:
                            dve.wait_ge(y_done, nth(tb, 1, 0))
                            dve.wait_ge(xr_in, nth(tb, 16, 15))
                            dve.wait_ge(x1_out, x1_stored(tb))
                            dve.tensor_tensor(flat(res[:, :, :]), p_bank[1][:, :], flat(xr[:, :, :]),
                                              ALU.add).then_inc(res_done, 1)
                            dve.wait_ge(res_done, nth(tb, 1, 0))
                        layernorm_part(tb, ts, 0)
                        if live(b, s - LAG_COPY) and (s - LAG_COPY) % 2 == 1:
                            k = s - LAG_COPY
                            dve.wait_ge(pt_done, nth(b, H, k))
                            wait_nth(dve, pv_done, b, H, k - NPT)
                            dve.tensor_copy(pt_sb[k % NPT][:, :], t_bank[k % 2][:, 0:3 * P]).then_inc(pt_sb_dve, 1)
                        if live(b, s):
                            i = s % NPB
                            wait_nth(dve, pt_done, b, H, s - NPB)
                            dve.wait_ge(scores_done, nth(b, H, s))
                            hold(dve, dve_passed)
                            for j, (dst, src) in enumerate(((slice(0, P), slice(0, P)), (slice(P, 3 * P), slice(T, 2 * T)))):
                                dve.tensor_tensor_reduce(probs[i][:, dst], s_bank[s % 2][:, src], mask[:, dst],
                                                         1.0, MASKED, ALU.add, ALU.max,
                                                         row_max[:, i, j:j + 1]).then_inc(masked, 1)
                            dve.wait_ge(masked, nth(b, 2 * H, 2 * s + 1))
                            dve.tensor_scalar(neg_max[:, i, :], row_max[:, i, :], -SCALE, None,
                                              ALU.mult).then_inc(neg_done, 1)
                        if live(b, s - 1):
                            row_inverse(b, s - 1)
                        if not is_last(b):
                            if s == XT_AT + 1:
                                xt_low(b + 1)
                            if s == KV_AT + 1:
                                k_low(b + 1)
                            if s == Q_AT + 1:
                                q_low(b + 1)
                        layernorm_part(tb, ts, 1)
                        if ts == LAG_PV:
                            yt_low(tb, 1)
                        if s == LAG_PV + HPT:
                            yt_low(b, 0)
                        if is_last(b) and s == B_LN_AT:
                            dve.wait_ge(shared.xp_in, 16)
                        if is_last(b) and B_LN_AT <= s < B_LN_AT + LN_STAGES // 2:
                            for stage in (2 * (s - B_LN_AT), 2 * (s - B_LN_AT) + 1):
                                layernorm_stage(dve, stage, 0, xs, xs, shared.ln_p, shared.ln_p_done, dve_passed)
                        if is_last(b) and s == B_PARTS_AT:
                            split_parts(dve, 0, xs, xt_hi, xt_lo, shared)
                walk_batches(dve, body)

            @block.tensor
            def _(pe):
                def transpose_x(nb):
                    pe.wait_ge(x_in, nth(nb, 16, 15))
                    if is_first(nb):
                        pe.wait_ge(consts_in, 16)
                    else:
                        pe.wait_ge(masked, nth(nb - 1, 2 * H, 2 * (XT_AT - 2) + 1))
                    transpose_tokens(pe, xs, p_bank[1], ident).then_inc(xt_done, 1)

                def project(out, m):
                    for k in range(KC):
                        ins = three_passes(pe, out, wa_hi[:, k, m:m + P], wa_lo[:, k, m:m + P], xt_hi[:, k, :],
                                           xt_lo[:, k, :], start=(k == 0), stop=(k == KC - 1))
                    return ins

                def project_kv(nb):
                    pe.wait_ge(xt_lo_done, nth(nb, 1, 0))
                    if is_first(nb):
                        pe.wait_ge(w_split, KC)
                    else:
                        pe.wait_ge(v_done, nth(nb - 1, 1, 0))
                    project(p_bank[0][:, 0:T], 0).then_inc(kv_proj, 1)

                def project_q(nb):
                    for t in range(TT):
                        ins = project(p_bank[1][:, t * T:t * T + T], 2 * VC + t * P)
                    ins.then_inc(q_proj, 1)

                def transpose_v(nb):
                    pe.wait_ge(vt_done, nth(nb, 1, 0))
                    pe.wait_ge(k_lo_done, nth(nb, 1, 0))
                    hold(pe, pe_passed)
                    for tt in range(TT):
                        ins = pe.transpose(p_bank[0][:, tt * VC:tt * VC + VC], vt[:, tt * P:tt * P + P],
                                           ident[0:VC, 0:VC])
                    ins.then_inc(v_psum, 1)

                def project_out(tb):
                    pe.wait_ge(yt_lo_done, nth(tb, 2, 1))
                    if is_first(tb):
                        pe.wait_ge(w_split, KC + 1)
                    if isinstance(tb, int) and tb >= NB - 2:
                        pe.wait_ge(res_done, nth(tb - 1, 1, 0))
                    else:
                        pe.wait_ge(q_lo_done, nth(tb + 2, 1, 0))
                    for tt in range(TT):
                        tok = slice(tt * P, tt * P + P)
                        for k in range(KC):
                            ins = three_passes(pe, p_bank[1][:, tt * C:tt * C + C], yt_hi[:, k, tok], yt_lo[:, k, tok],
                                               wo_hi[:, k, :], wo_lo[:, k, :], start=(k == 0), stop=(k == KC - 1))
                    ins.then_inc(y_done, 1)

                def weigh_values(b, k):
                    h = k % H
                    t, hh, g = h // HPT, h % HPT, h * KVA // H
                    copied = (pt_sb_act, pt_sb_dve)[k % 2]
                    pe.wait_ge(copied, nth(b, H // 2, (k - k % 2) // 2))
                    if h % (H // KVA) == 0:
                        pe.wait_ge(v_pad_done, nth(b, KVA, (k - h) // H * KVA + g))
                    if hh == 0:
                        wait_nth(pe, yt_lo_done, b, 2, ((k - h) // H - 1) * 2 + t)
                    o, pt, at = o_bank[t], pt_sb[k % NPT], P - HSA - HSA * hh
                    pe.matmul(o[:, 0:T], v_pad[:, 0, g, at:at + P], pt[:, 0:T], start=(hh == 0), stop=False,
                              skip_group_check=True)
                    pe.matmul(o[:, P:T], v_pad[:, 1, g, at:at + P], pt[:, T:3 * P], start=False,
                              stop=(hh == HPT - 1), skip_group_check=True).then_inc(pv_done, 1)

                def body(b):
                    if is_first(b):
                        transpose_x(0)
                        project_kv(0)
                        project_q(0)
                        transpose_v(0)
                    for s in steps(b):
                        if live(b, s):
                            if s % HPT == 0:
                                pe.wait_ge(k_in[s // HPT], nth(b, 16 * KS, 16 * KS - 1))
                                pe.wait_ge(q_in[s // HPT], nth(b, 16 * QS, 16 * QS - 1))
                            wait_nth(pe, masked, b, 2 * H, 2 * (s - 2) + 1)
                            for tt in range(TT):
                                ins = pe.matmul(s_bank[s % 2][:, tt * T:tt * T + T],
                                                q_stack[:, s // 2, tt * P:tt * P + P],
                                                k_stack[s % 2][:, s * KVA // H, :], start=True, stop=True)
                            ins.then_inc(scores_done, 1)
                        if live(b, s - LAG_PV):
                            weigh_values(b, s - LAG_PV)
                        if live(b, s - LAG_T):
                            k = s - LAG_T
                            pe.wait_ge(probs_done, nth(b, H, k))
                            copied = (pt_sb_act, pt_sb_dve)[k % 2]
                            if live(b, k - 2):
                                pe.wait_ge(copied, nth(b, H // 2, (k - 2 - k % 2) // 2))
                            for c in range(3):
                                ins = pe.transpose(t_bank[k % 2][:, c * P:c * P + P], probs[k % NPB][:, c * P:c * P + P], ident)
                            ins.then_inc(pt_done, 1)
                        tb, ts = tail_of(b, s)
                        if ts == LAG_PV + 2:
                            project_out(tb)
                        if is_last(b) and s == B_XT_AT:
                            pe.wait_ge(shared.ln_p_done, LN_STEPS)
                            pe.wait_ge(res_done, NB - 1)
                            transpose_tokens(pe, xs, p_bank[1], ident).then_inc(shared.xpt_done, 1)
                        if not is_last(b):
                            if s == XT_AT:
                                transpose_x(b + 1)
                            if s == KV_AT:
                                project_kv(b + 1)
                            if s == Q_AT:
                                project_q(b + 1)
                            if s == VT_AT:
                                transpose_v(b + 1)
                walk_batches(pe, body)


def layer_b(nc, x1, w_out, w_moe, rows_dram, out, shared):
    w_qkv_hi, w_qkv_lo, consts, cols = shared.w_hi, shared.w_lo, shared.consts, shared.cols
    ht_hi, ht_lo, ln_p = shared.xt_hi, shared.xt_lo, shared.ln_p
    xp_in, xpt_done, ht_done, ht_parts, ln_p_done = (
        shared.xp_in, shared.xpt_done, shared.ht_done, shared.ht_parts, shared.ln_p_done)
    SCALE = HSB ** -0.5
    HALF = HSB // 2
    LEAD = 3
    LAG_T, LAG_PV, LAG_O = 1, 2, 3
    TAIL_STEPS = 26
    NPB = 2
    VPAIRS = H // 2
    WO_CH = KC * T
    N_WO = H * C // WO_CH
    SEGS = (slice(0, P), slice(P, 3 * P))
    ROUTE = {9: ((0,), (1,), (), ()), 10: ((2,), (3, 4), (5, 6), (7, 8)), 11: ((9,), (10, 11), (12, 13), (14,)),
             12: ((15,), (), (), ()), 13: ((), (16,), (17, 18), (19, 20))}
    N_ROUTE = 21
    ALL = tuple(range(E))
    UP_AT = {11: (0, 1), 15: (2, 3)}, {8: ALL}
    GELU_AT = {12: (0, 1), 16: (2, 3)}, {12: ALL}
    DOWN_AT = {13: (0, 1), 17: (2, 3)}, {13: ALL}
    MIX_AT = {14: (0, 1), 18: (2, 3)}, {14: ALL}
    LN_O_AT_LAST = 15
    LN_P_AT, LN_H_AT, LN_O_AT = 5, 3, 20
    R_SHIFTED, R_GAP = 1, 15

    with ExitStack() as ctx:
        def sb(name, shape, dt=F32):
            return ctx.enter_context(nc.sbuf_tensor("b_" + name, shape, dt))

        def bank(name):
            return ctx.enter_context(nc.psum_tensor("b_" + name, [P, 512], F32))

        def sem(name):
            return ctx.enter_context(nc.semaphore("b_" + name))

        def ln_buffers(n):
            return sb(f"stats_{n}", [P, TT, 6]), sb(f"mv_{n}", [P, TT, 2]), sb(f"work_{n}", [P, 3, TT])

        wo_hi, wo_lo = (sb(n, [P, H, C], F32R) for n in ("wo_hi", "wo_lo"))
        w_up = sb("w_up", [P, E, KC, C])
        w_down = sb("w_down", [P, E, KC, C])
        rows = sb("rows", [P, NROWS])
        xp = sb("xp", [P, TT, C])
        xt = sb("xt", [P, TT, C])
        h_sb = sb("h_sb", [P, TT, C])
        xn = sb("xn", [P, TT, C])
        mix = sb("mix", [P, TT, C])
        zp = sb("zp", [P, TT, C])
        zt = xn
        ht, h2t = sb("ht", [P, KC, T]), sb("h2t", [P, KC, T])
        qk = [sb(f"qk{i}", [P, 2, T]) for i in range(2)]
        qk_swap = [sb(f"qk_swap{i}", [P, 2, T]) for i in range(2)]
        qk_rot = [sb(f"qk_rot{i}", [P, 2, T]) for i in range(2)]
        v_sb = [sb(f"v_sb{i}", [P, TT, 2, HSB]) for i in range(2)]
        probs = [sb(f"probs{i}", [P, 3 * P]) for i in range(NPB)]
        neg_max, row_max, row_sum, row_inv = (
            sb(n, [P, NPB, 2]) for n in ("neg_max", "row_max", "row_sum", "row_inv"))
        pt_sb = [sb(f"pt_sb{i}", [P, 3 * P]) for i in range(2)]
        ot_hi, ot_lo = ([sb(f"{n}{i}", [P, T], F32R) for i in range(2)] for n in ("ot_hi", "ot_lo"))
        units = [sb(f"units{i}", [P, KC, T]) for i in range(2)]
        ln_h, ln_o = (ln_buffers(n) for n in "ho")
        first, total, inv_total, second, gap, share = (sb(n, [P, TT, 1]) for n in (
            "first", "total", "inv_total", "second", "gap", "share"))
        shifted, expd, raw, rank, is_top, is_second, picked, comb = (sb(n, [P, TT, E]) for n in (
            "shifted", "expd", "raw", "rank", "is_top", "is_second", "picked", "comb"))
        above, equal = sb("above", [P, TT, E, E]), sb("equal", [P, TT, E, E])

        qk_bank, v_bank, s_bank, t_bank, o_bank, y_bank = (
            bank(n) for n in ("qk", "v", "scores", "p_t", "o_t", "y"))
        m_bank = [bank(f"moe{i}") for i in range(2)]

        params_in, moe_in = sem("params_in"), sem("moe_in")
        wo_in = [sem(f"wo_in{i}") for i in range(2)]
        wo_hi_done, wo_lo_done = sem("wo_hi_done"), sem("wo_lo_done")
        xt_in = sem("xt_in")
        ln_h_done, ln_o_done = sem("ln_h_done"), sem("ln_o_done")
        qk_proj, qk_done, rope_done, rot_done = sem("qk_proj"), sem("qk_done"), sem("rope_done"), sem("rot_done")
        swap_in = [sem(f"swap_in{i}") for i in range(2)]
        v_proj, v_done = sem("v_proj"), sem("v_done")
        scores_done, masked, neg_done = sem("scores_done"), sem("masked"), sem("neg_done")
        exp_done, inv_done, probs_done = sem("exp_done"), sem("inv_done"), sem("probs_done")
        pt_done, pt_copied, pv_done = sem("pt_done"), sem("pt_copied"), sem("pv_done")
        ot_hi_done, ot_lo_done, o_proj = sem("ot_hi_done"), sem("ot_lo_done"), sem("o_proj")
        hb_done, h_done = sem("hb_done"), sem("h_done")
        h2t_psum, h2t_done, logits_psum = sem("h2t_psum"), sem("h2t_done"), sem("logits_psum")
        route, route_exp = sem("route"), sem("route_exp")
        up_done, units_done, down_done, mixed = sem("up_done"), sem("units_done"), sem("down_done"), sem("mixed")
        bias_done, sum_done, stored = sem("bias_done"), sem("sum_done"), sem("stored")
        dve_passed = sem("dve_passed")

        x1_view = x1.rearrange("b (t p) c -> b p t c", p=P)
        out_view = out.rearrange("b (t p) c -> b p t c", p=P)
        ident, mask = const(consts, "ident"), const(consts, "mask_b")
        cos = const(consts, "cos").unsqueeze(1).broadcast_to([P, 2, T])
        sin = const(consts, "sin").unsqueeze(1).broadcast_to([P, 2, T])
        before = const(consts, "before").rearrange("p (i j) -> p i j", i=E)

        def col(name, i=0):
            return column(cols, name, i)

        def row(name, i=0):
            a = ROWS[name][0] + i * C
            return rows[:, a:a + C].unsqueeze(1).broadcast_to([P, TT, C])

        def steps(b):
            return range(-LEAD if is_first(b) else 0, H + TAIL_STEPS if is_last(b) else H)

        def tails(b, s):
            for j in range(3):
                ts = s + (j - 1) * H
                if 0 <= ts < TAIL_STEPS and not (isinstance(b, int) and b < j):
                    yield b - j, ts

        def experts_at(when, tb, ts):
            return when[is_last(tb)].get(ts, ())

        def bank_of(tb, e):
            return (qk_bank, v_bank)[e - 2] if is_last(tb) and e >= 2 else m_bank[e % 2]

        def units_of(tb, e):
            return qk[e - 2] if is_last(tb) and e >= 2 else units[e % 2]

        def logits_bank(tb):
            return t_bank if is_last(tb) else m_bank[1]

        def walk(eng, body):
            body(0)
            body(1)
            with eng.Fori(2, NB - 1) as b:
                body(b)
            body(NB - 1)

        def wait_swap(eng, b, k):
            eng.wait_ge(swap_in[k % 2], b * (2 * 16 * H // 2) + 2 * 16 * (k // 2 + 1))

        with nc.Block() as block:
            @block.sync
            def _(sp):
                sp.dma_start(rows[:, :], rows_dram).then_inc(params_in, 16)

                def load_w_out(c):
                    if c >= 2:
                        sp.wait_ge(wo_lo_done, c - 1)
                    sp.dma_start(flat(units[c % 2][:, :, :]), w_out[:, c * WO_CH:(c + 1) * WO_CH])\
                      .then_inc(wo_in[c % 2], 16)

                def load_w_moe():
                    n = E * KC * C
                    sp.dma_start(w_up[:, :, :, :].rearrange("p e k n -> p (e k n)"), w_moe[:, 0:n])\
                      .then_inc(moe_in, 16)
                    sp.dma_start(w_down[:, :, :, :].rearrange("p e k n -> p (e k n)"), w_moe[:, n:2 * n])\
                      .then_inc(moe_in, 16)

                def body(b):
                    for s in steps(b):
                        if live(b, s + 2):
                            k = s + 2
                            sp.wait_ge(qk_done, nth(b, 2 * H, 2 * k + 1))
                            for lo, hi in ((0, HALF), (HALF, 0)):
                                sp.dma_start(qk_swap[k % 2][lo:lo + HALF, :, :], qk[k % 2][hi:hi + HALF, :, :])\
                                  .then_inc(swap_in[k % 2], 16)
                        if is_first(b) and s + LEAD < N_WO:
                            load_w_out(s + LEAD)
                        if is_first(b) and s + LEAD == N_WO:
                            load_w_moe()
                        if s == 1 and not is_last(b):
                            sp.wait_ge(xpt_done, nth(b, 1, 0))
                            if is_first(b):
                                sp.wait_ge(shared.x1_out, x1_stored(NB))
                            sp.dma_start(xp[:, :, :], x1_view[b + 1]).then_inc(xp_in, 16)
                        if s == 15:
                            if not is_first(b):
                                sp.wait_ge(bias_done, nth(b - 1, 2 * E, 1))
                            sp.dma_start(xt[:, :, :], x1_view[b]).then_inc(xt_in, 16)
                        for tb, ts in tails(b, s):
                            if ts == TAIL_STEPS - 1:
                                sp.wait_ge(ln_o_done, nth(tb, LN_STEPS, LN_STEPS - 1))
                                sp.dma_start(out_view[tb], mix[:, :, :]).then_inc(stored, 16)
                walk(sp, body)
                sp.wait_ge(stored, 16 * NB)

            @block.gpsimd
            def _(pool):
                def add_out_bias(tb):
                    pool.wait_ge(xt_in, nth(tb, 16, 15))
                    if is_first(tb):
                        pool.wait_ge(params_in, 16)
                    else:
                        pool.wait_ge(mixed, nth(tb - 1, E * TT, TT - 1))
                    pool.tensor_tensor(h_sb[:, :, :], xt[:, :, :], row("bo"), ALU.add).then_inc(hb_done, 1)

                def add_expert_bias(tb, e):
                    if e == 0:
                        pool.wait_ge(route, nth(tb, N_ROUTE, N_ROUTE - 1))
                        if not is_first(tb):
                            pool.wait_ge(sum_done, nth(tb - 1, 1, 0))
                    wait_nth(pool, bias_done, tb, 2 * E, 2 * e - 1)
                    pool.tensor_tensor(zt[:, :, :], row("be2", e), comb[:, :, e:e + 1].broadcast_to([P, TT, C]),
                                       ALU.mult).then_inc(bias_done, 1)
                    pool.wait_ge(bias_done, nth(tb, 2 * E, 2 * e))
                    pool.tensor_tensor(zp[:, :, :], (xt if e == 0 else zp)[:, :, :], zt[:, :, :], ALU.add)\
                        .then_inc(bias_done, 1)

                def body(b):
                    for s in steps(b):
                        if live(b, s):
                            i = s % NPB
                            pool.wait_ge(inv_done, nth(b, H, s))
                            for j, seg in enumerate(SEGS):
                                n = seg.stop - seg.start
                                ins = pool.tensor_tensor(probs[i][:, seg], probs[i][:, seg],
                                                         row_inv[:, i, j:j + 1].broadcast_to([P, n]), ALU.mult)
                            ins.then_inc(probs_done, 1)
                        if live(b, s + 2):
                            k = s + 2
                            pool.wait_ge(rope_done, nth(b, 2 * H, 2 * k + 1))
                            wait_nth(pool, scores_done, b, H, k - 2)
                            pool.tensor_tensor(qk_rot[k % 2][:, :, :], qk[k % 2][:, :, :],
                                               qk_swap[k % 2][:, :, :], ALU.add).then_inc(rot_done, 1)
                        for tb, ts in tails(b, s):
                            if ts == 1:
                                add_out_bias(tb)
                            if 14 <= ts < 14 + E:
                                add_expert_bias(tb, ts - 14)
                walk(pool, body)

            @block.scalar
            def _(act):
                def affine(dst, src, name, done):
                    for k in range(KC):
                        act.activation(dst[:, k, :], src[:, k * T:k * T + T], ACT.Identity,
                                       bias=col(name + "_b", k), scale=col(name + "_w", k)).then_inc(done, 1)

                def prepare(nb):
                    act.wait_ge(xpt_done, nth(nb, 1, 0))
                    act.wait_ge(ht_parts, nth(nb - 1, 2, 1))
                    affine(ht, m_bank[0], "ln1", ht_done)

                def gelu(tb, e):
                    act.wait_ge(up_done, nth(tb, E, e))
                    if e < 2 or not is_last(tb):
                        wait_nth(act, down_done, tb, E, e - 2)
                    for i in range(KC):
                        act.activation(units_of(tb, e)[:, i, :], bank_of(tb, e)[:, i * T:i * T + T], ACT.Gelu,
                                       bias=col("be1", KC * e + i)).then_inc(units_done, 1)

                def body(b):
                    for s in steps(b):
                        if live(b, s + 2):
                            k = s + 2
                            act.wait_ge(qk_proj, nth(b, H, k))
                            wait_nth(act, rot_done, b, H, k - 2)
                            for j, name in enumerate(("bq", "bk")):
                                act.activation(qk[k % 2][:, j, :], qk_bank[:, j * T:j * T + T], ACT.Identity,
                                               bias=col(name, k % H)).then_inc(qk_done, 1)
                        if live(b, s):
                            i = s % NPB
                            act.wait_ge(neg_done, nth(b, H, s))
                            for j, seg in enumerate(SEGS):
                                ins = act.activation(probs[i][:, seg], probs[i][:, seg], ACT.Exp,
                                                     bias=neg_max[:, i, j:j + 1], scale=SCALE,
                                                     accum_out=row_sum[:, i, j:j + 1])
                            ins.then_inc(exp_done, 1)
                        if live(b, s - LAG_PV):
                            k = s - LAG_PV
                            act.wait_ge(pv_done, nth(b, H, k))
                            wait_nth(act, o_proj, b, H, k - 2)
                            act.activation(ot_hi[k % 2][:, :], o_bank[:, 0:T], ACT.Identity,
                                           bias=col("bv", k % H)).then_inc(ot_hi_done, 1)
                        if live(b, s - LAG_T):
                            k = s - LAG_T
                            act.wait_ge(pt_done, nth(b, H, k))
                            wait_nth(act, pv_done, b, H, k - 2)
                            act.activation(pt_sb[k % 2][:, :], t_bank[:, 0:3 * P], ACT.Copy).then_inc(pt_copied, 1)
                        if s % 2 == 1 and live(b, s + 1):
                            k = s + 1
                            act.wait_ge(v_proj, nth(b, VPAIRS, k // 2))
                            wait_nth(act, pv_done, b, H, k - 3)
                            act.activation(v_sb[k // 2 % 2][:, :, :, :].rearrange("p t h d -> p (t h d)"),
                                           v_bank[:, :], ACT.Copy).then_inc(v_done, 1)
                        c = s + 2
                        if is_first(b) and 0 <= c < N_WO:
                            act.wait_ge(wo_in[c % 2], 16 * (c // 2 + 1))
                            act.activation(wo_hi[:, :, :].rearrange("p h c -> p (h c)")[:, c * WO_CH:(c + 1) * WO_CH],
                                           flat(units[c % 2][:, :, :]), ACT.Copy).then_inc(wo_hi_done, 1)
                        if s == 8 and not is_last(b):
                            prepare(b + 1)
                        for tb, ts in tails(b, s):
                            if ts == 7:
                                act.wait_ge(h2t_psum, nth(tb, 1, 0))
                                affine(h2t, m_bank[0], "ln2", h2t_done)
                            if ts == 9:
                                act.wait_ge(route, nth(tb, N_ROUTE, R_SHIFTED))
                                act.activation(expd[:, :, :], shifted[:, :, :], ACT.Exp).then_inc(route_exp, 1)
                            if ts == 12:
                                act.wait_ge(route, nth(tb, N_ROUTE, R_GAP))
                                act.activation(gap[:, :, :], gap[:, :, :], ACT.Exp).then_inc(route_exp, 1)
                            for e in experts_at(GELU_AT, tb, ts):
                                gelu(tb, e)
                walk(act, body)

            @block.vector
            def _(dve):
                def split_ht(nb):
                    dve.wait_ge(qk_proj, nth(nb - 1, H, H - 1))
                    dve.wait_ge(v_proj, nth(nb - 1, VPAIRS, VPAIRS - 1))
                    split_parts(dve, nb, ht, ht_hi, ht_lo, shared)

                def route_step(tb, n):
                    if n == 0:
                        dve.wait_ge(logits_psum, nth(tb, 1, 0))
                        if not is_first(tb):
                            dve.wait_ge(bias_done, nth(tb - 1, 2 * E, 2 * E - 1))
                    else:
                        dve.wait_ge(route, nth(tb, N_ROUTE, n - 1))
                    if n == R_SHIFTED + 1:
                        dve.wait_ge(route_exp, nth(tb, 2, 0))
                    if n == R_GAP + 1:
                        dve.wait_ge(route_exp, nth(tb, 2, 1))
                    logits = logits_bank(tb)[:, 0:TT * E].rearrange("p (t e) -> p t e", t=TT)

                    def over_experts(ap):
                        return ap[:, :, :].broadcast_to([P, TT, E])

                    def by_row(ap):
                        return ap[:, :, :].unsqueeze(3).broadcast_to([P, TT, E, E])

                    def by_column(ap):
                        return ap[:, :, :].unsqueeze(2).broadcast_to([P, TT, E, E])

                    if n == 0:
                        ins = dve.tensor_reduce(first[:, :, 0], logits, AX.X, ALU.max)
                    elif n == 1:
                        ins = dve.tensor_tensor(shifted[:, :, :], logits, over_experts(first), ALU.subtract)
                    elif n == 2:
                        ins = dve.tensor_reduce(total[:, :, 0], expd[:, :, :], AX.X, ALU.add)
                    elif n == 3:
                        ins = dve.reciprocal(inv_total[:, :, :], total[:, :, :])
                    elif n == 4:
                        ins = dve.tensor_tensor(raw[:, :, :], expd[:, :, :], over_experts(inv_total), ALU.mult)
                    elif n == 5:
                        ins = dve.tensor_tensor(above[:, :, :, :], by_column(raw), by_row(raw), ALU.is_gt)
                    elif n == 6:
                        ins = dve.tensor_tensor(equal[:, :, :, :], by_column(raw), by_row(raw), ALU.is_equal)
                    elif n == 7:
                        ins = dve.tensor_tensor(equal[:, :, :, :], equal[:, :, :, :],
                            before.unsqueeze(1).broadcast_to([P, TT, E, E]), ALU.mult)
                    elif n == 8:
                        ins = dve.tensor_tensor(above[:, :, :, :], above[:, :, :, :], equal[:, :, :, :], ALU.add)
                    elif n == 9:
                        ins = dve.tensor_reduce(rank[:, :, :], above[:, :, :, :], AX.X, ALU.add)
                    elif n == 10:
                        ins = dve.tensor_scalar(is_top[:, :, :], rank[:, :, :], 0.0, None, ALU.is_equal)
                    elif n == 11:
                        ins = dve.tensor_scalar(is_second[:, :, :], rank[:, :, :], 1.0, None, ALU.is_equal)
                    elif n == 12:
                        ins = dve.tensor_reduce(first[:, :, 0], raw[:, :, :], AX.X, ALU.max)
                    elif n == 13:
                        ins = dve.tensor_tensor(picked[:, :, :], raw[:, :, :], is_second[:, :, :], ALU.mult)
                    elif n == 14:
                        ins = dve.tensor_reduce(second[:, :, 0], picked[:, :, :], AX.X, ALU.add)
                    elif n == 15:
                        ins = dve.tensor_tensor(gap[:, :, :], second[:, :, :], first[:, :, :], ALU.subtract)
                    elif n == 16:
                        ins = dve.tensor_scalar(share[:, :, :], gap[:, :, :], 1.0, None, ALU.add)
                    elif n == 17:
                        ins = dve.reciprocal(share[:, :, :], share[:, :, :])
                    elif n == 18:
                        ins = dve.tensor_tensor(picked[:, :, :], is_second[:, :, :], over_experts(gap), ALU.mult)
                    elif n == 19:
                        ins = dve.tensor_tensor(picked[:, :, :], picked[:, :, :], is_top[:, :, :], ALU.add)
                    elif n == 20:
                        ins = dve.tensor_tensor(comb[:, :, :], picked[:, :, :], over_experts(share), ALU.mult)
                    ins.then_inc(route, 1)

                def mix_expert(tb, e):
                    dve.wait_ge(down_done, nth(tb, E, e))
                    if e:
                        dve.wait_ge(mixed, nth(tb, E * TT, TT * e - 1))
                    else:
                        dve.wait_ge(route, nth(tb, N_ROUTE, N_ROUTE - 1))
                        if not is_first(tb):
                            dve.wait_ge(stored, nth(tb - 1, 16, 15))
                    for tt in range(TT):
                        dve.scalar_tensor_tensor(out=mix[:, tt, :], in0=bank_of(tb, e)[:, tt * C:tt * C + C],
                                                 scalar=comb[:, tt, e:e + 1], in1=(mix if e else h_sb)[:, tt, :],
                                                 op0=ALU.mult, op1=ALU.add).then_inc(mixed, 1)

                def spread(s, at, n, slot):
                    part = 4 * (s - at) + slot
                    return (part,) if at <= s and part < n else ()

                def slot_work(b, s, slot):
                    if not is_last(b):
                        if s == LN_P_AT and slot == 0:
                            dve.wait_ge(xp_in, nth(b + 1, 16, 15))
                        for part in spread(s, LN_P_AT, LN_STAGES, slot):
                            layernorm_stage(dve, part, b + 1, xp, xp, ln_p, ln_p_done, dve_passed)
                    for tb, ts in tails(b, s):
                        if ts == LN_H_AT and slot == 0:
                            dve.wait_ge(h_done, nth(tb, 1, 0))
                        for part in spread(ts, LN_H_AT, LN_STAGES, slot):
                            layernorm_stage(dve, part, tb, h_sb, xn, ln_h, ln_h_done, dve_passed)
                        for n in ROUTE.get(ts, ((),) * 4)[slot]:
                            route_step(tb, n)
                        ln_o_at = LN_O_AT_LAST if is_last(tb) else LN_O_AT
                        if ts == ln_o_at and slot == 0:
                            dve.wait_ge(bias_done, nth(tb, 2 * E, 2 * E - 1))
                            dve.wait_ge(mixed, nth(tb, E * TT, E * TT - 1))
                            dve.tensor_tensor(mix[:, :, :], mix[:, :, :], zp[:, :, :], ALU.add).then_inc(sum_done, 1)
                            dve.wait_ge(sum_done, nth(tb, 1, 0))
                        for part in spread(ts, ln_o_at, LN_STAGES, slot):
                            layernorm_stage(dve, part, tb, mix, mix, ln_o, ln_o_done, dve_passed)

                def body(b):
                    for s in steps(b):
                        if s == 13 and not is_last(b):
                            split_ht(b + 1)
                        if live(b, s):
                            i = s % NPB
                            wait_nth(dve, pt_done, b, H, s - NPB)
                            dve.wait_ge(scores_done, nth(b, H, s))
                            hold(dve, dve_passed)
                            for j, seg in enumerate(SEGS):
                                dve.tensor_tensor_reduce(probs[i][:, seg], s_bank[:, seg], mask[:, seg], 1.0, MASKED,
                                                         ALU.add, ALU.max, row_max[:, i, j:j + 1]).then_inc(masked, 1)
                            dve.wait_ge(masked, nth(b, 2 * H, 2 * s + 1))
                            dve.tensor_scalar(neg_max[:, i, :], row_max[:, i, :], -SCALE, None, ALU.mult)\
                               .then_inc(neg_done, 1)
                        slot_work(b, s, 0)
                        slot_work(b, s, 1)
                        if live(b, s - LAG_PV):
                            k = s - LAG_PV
                            dve.wait_ge(ot_hi_done, nth(b, H, k))
                            dve.scalar_tensor_tensor(out=ot_lo[k % 2][:, :], in0=o_bank[:, 0:T],
                                                     scalar=col("bv", k % H), in1=ot_hi[k % 2][:, :].bitcast(F32),
                                                     op0=ALU.add, op1=ALU.subtract).then_inc(ot_lo_done, 1)
                        if live(b, s):
                            dve.wait_ge(exp_done, nth(b, H, s))
                            dve.reciprocal(row_inv[:, s % NPB, :], row_sum[:, s % NPB, :]).then_inc(inv_done, 1)
                        for tb, ts in tails(b, s):
                            if ts == LAG_O - 1:
                                dve.wait_ge(o_proj, nth(tb, H, H - 1))
                                dve.wait_ge(hb_done, nth(tb, 1, 0))
                                dve.tensor_tensor(flat(h_sb[:, :, :]), y_bank[:, :], flat(h_sb[:, :, :]), ALU.add)\
                                   .then_inc(h_done, 1)
                        for tb, ts in tails(b, s):
                            for e in experts_at(MIX_AT, tb, ts):
                                mix_expert(tb, e)
                        slot_work(b, s, 2)
                        if live(b, s + 2):
                            k = s + 2
                            wait_swap(dve, b, k)
                            dve.tensor_tensor(qk_swap[k % 2][:, :, :], qk_swap[k % 2][:, :, :], sin, ALU.mult)\
                               .then_inc(rope_done, 1)
                            dve.tensor_tensor(qk[k % 2][:, :, :], qk[k % 2][:, :, :], cos, ALU.mult)\
                               .then_inc(rope_done, 1)
                        slot_work(b, s, 3)
                        c = s + 2
                        if is_first(b) and 0 <= c < N_WO:
                            dve.wait_ge(wo_hi_done, c + 1)
                            at = slice(c * WO_CH, (c + 1) * WO_CH)
                            dve.tensor_tensor(wo_lo[:, :, :].rearrange("p h c -> p (h c)")[:, at],
                                              flat(units[c % 2][:, :, :]),
                                              wo_hi[:, :, :].rearrange("p h c -> p (h c)")[:, at].bitcast(F32),
                                              ALU.subtract).then_inc(wo_lo_done, 1)
                walk(dve, body)

            @block.tensor
            def _(pe):
                def prepare(nb):
                    pe.wait_ge(ln_p_done, nth(nb, LN_STEPS, LN_STEPS - 1))
                    if not (isinstance(nb, int) and nb == 1):
                        pe.wait_ge(h2t_done, nth(nb - 2, KC, KC - 1))
                    transpose_tokens(pe, xp, m_bank[0], ident).then_inc(xpt_done, 1)

                def project_qk(b, k):
                    if k % H == 0:
                        pe.wait_ge(ht_parts, nth(b, 2, k // H * 2 + 1))
                    wait_nth(pe, qk_done, b, 2 * H, 2 * (k - 1) + 1)
                    for j in range(2):
                        for c in range(KC):
                            at = (j * KC + c) * H * HSB + (k % H) * HSB
                            ins = three_passes(pe, qk_bank[:, j * T:j * T + T], w_qkv_hi[:, at:at + HSB],
                                               w_qkv_lo[:, at:at + HSB], ht_hi[:, c, :], ht_lo[:, c, :],
                                               start=(c == 0), stop=(c == KC - 1))
                    ins.then_inc(qk_proj, 1)

                def project_v(b, k):
                    wait_nth(pe, v_done, b, VPAIRS, k // 2 - 1)
                    for tt in range(TT):
                        tok = slice(tt * P, tt * P + P)
                        for c in range(KC):
                            at = (2 * KC + c) * H * HSB + (k % H) * HSB
                            ins = three_passes(pe, v_bank[:, tt * 2 * HSB:(tt + 1) * 2 * HSB], ht_hi[:, c, tok],
                                               ht_lo[:, c, tok], w_qkv_hi[:, at:at + 2 * HSB],
                                               w_qkv_lo[:, at:at + 2 * HSB], start=(c == 0), stop=(c == KC - 1))
                    ins.then_inc(v_proj, 1)

                def expert(tb, e, down):
                    bank_, done = bank_of(tb, e), down_done if down else up_done
                    if down:
                        pe.wait_ge(units_done, nth(tb, E * KC, KC * e + KC - 1))
                    elif e >= 2 and is_last(tb):
                        pe.wait_ge(*((qk_done, NB * 2 * H), (v_done, NB * VPAIRS))[e - 2])
                    elif e >= 2:
                        pe.wait_ge(mixed, nth(tb, E * TT, TT * (e - 1) - 1))
                    for i in range(2):
                        for c in range(KC):
                            if down:
                                args = units_of(tb, e)[:, c, i * P:i * P + P], w_down[:, e, c, :]
                            else:
                                args = w_up[:, e, c, i * P:i * P + P], h2t[:, c, :]
                            ins = pe.matmul(bank_[:, i * T:i * T + T], *args, start=(c == 0), stop=(c == KC - 1),
                                            skip_group_check=True)
                    ins.then_inc(done, 1)

                def body(b):
                    for s in steps(b):
                        if live(b, s):
                            pe.wait_ge(rot_done, nth(b, H, s))
                            wait_nth(pe, masked, b, 2 * H, 2 * (s - 1) + 1)
                            rot = qk_rot[s % 2]
                            for tt, seg in enumerate(SEGS):
                                ins = pe.matmul(s_bank[:, seg], rot[:, 0, tt * P:tt * P + P],
                                                rot[:, 1, 0:seg.stop - seg.start], start=True, stop=True)
                            ins.then_inc(scores_done, 1)
                        if live(b, s - LAG_O):
                            k = s - LAG_O
                            head = k % H
                            pe.wait_ge(ot_lo_done, nth(b, H, k))
                            if is_first(b) and 0 <= k < H:
                                pe.wait_ge(wo_lo_done, k * C // WO_CH + 1)
                            if head == 0 and not is_first(b):
                                pe.wait_ge(h_done, nth(b - 1, 1, 0))
                            for tt in range(TT):
                                tok = slice(tt * P, tt * P + P)
                                ins = three_passes(pe, y_bank[:, tt * C:tt * C + C], ot_hi[k % 2][:, tok],
                                                   ot_lo[k % 2][:, tok], wo_hi[:, head, :], wo_lo[:, head, :],
                                                   start=(head == 0 and tt == 0), stop=(head == H - 1))
                            ins.then_inc(o_proj, 1)
                        if live(b, s - LAG_PV):
                            k = s - LAG_PV
                            pe.wait_ge(pt_copied, nth(b, H, k))
                            if k % 2 == 0:
                                pe.wait_ge(v_done, nth(b, VPAIRS, k // 2))
                            wait_nth(pe, ot_lo_done, b, H, k - 1)
                            v, pt = v_sb[k // 2 % 2], pt_sb[k % 2]
                            pe.matmul(o_bank[:, 0:T], v[:, 0, k % 2, :], pt[:, 0:T], start=True, stop=False,
                                      skip_group_check=True)
                            pe.matmul(o_bank[:, P:T], v[:, 1, k % 2, :], pt[:, T:3 * P], start=False, stop=True,
                                      skip_group_check=True).then_inc(pv_done, 1)
                        for tb, ts in tails(b, s):
                            for e in experts_at(DOWN_AT, tb, ts):
                                expert(tb, e, down=True)
                        if live(b, s + LEAD):
                            project_qk(b, s + LEAD)
                        if live(b, s - LAG_T):
                            k = s - LAG_T
                            pe.wait_ge(probs_done, nth(b, H, k))
                            wait_nth(pe, pt_copied, b, H, k - 1)
                            for c in range(3):
                                ins = pe.transpose(t_bank[:, c * P:c * P + P], probs[k % NPB][:, c * P:c * P + P], ident)
                            ins.then_inc(pt_done, 1)
                        if s % 2 == 0 and live(b, s + 2):
                            project_v(b, s + 2)
                        if s == 8 and not is_last(b):
                            prepare(b + 1)
                        for tb, ts in tails(b, s):
                            if ts == 7:
                                pe.wait_ge(ln_h_done, nth(tb, LN_STEPS, LN_STEPS - 1))
                                if is_first(tb):
                                    pe.wait_ge(ht_done, nth(tb + 1, KC, KC - 1))
                                else:
                                    pe.wait_ge(mixed, nth(tb - 1, E * TT, E * TT - 1))
                                transpose_tokens(pe, xn, m_bank[0], ident).then_inc(h2t_psum, 1)
                            if ts == 8:
                                pe.wait_ge(h2t_done, nth(tb, KC, KC - 1))
                                if is_last(tb):
                                    pe.wait_ge(pt_copied, NB * H)
                                for tt in range(TT):
                                    for c in range(KC):
                                        a = COLS["w_gate"][0] + c * E
                                        ins = pe.matmul(logits_bank(tb)[:, tt * E:tt * E + E], h2t[:, c, tt * P:tt * P + P],
                                                        cols[:, a:a + E], start=(c == 0), stop=(c == KC - 1),
                                                        skip_group_check=True)
                                ins.then_inc(logits_psum, 1)
                            for e in experts_at(UP_AT, tb, ts):
                                if e == 0:
                                    pe.wait_ge(moe_in, 32)
                                    if not is_last(tb):
                                        pe.wait_ge(route, nth(tb, N_ROUTE, R_SHIFTED))
                                    if not (isinstance(tb, int) and tb >= NB - 2):
                                        pe.wait_ge(ht_done, nth(tb + 2, KC, KC - 1))
                                expert(tb, e, down=False)
                walk(pe, body)


class Shared:
    pass


def build(nc, x, w_attn_a, w_out_a, consts_dram, w_qkv, w_out_b, w_moe, cols_dram, rows_dram, out):
    x1 = nc.dram_tensor("x1", (NB, T, C), F32, kind="Internal").ap()
    with ExitStack() as ctx:
        def sb(name, shape, dt=F32):
            return ctx.enter_context(nc.sbuf_tensor(name, shape, dt))

        def sem(name):
            return ctx.enter_context(nc.semaphore(name))

        shared = Shared()
        shared.w_hi, shared.w_lo = (sb(n, [P, QKVW], F32R) for n in ("w_hi", "w_lo"))
        shared.consts, shared.cols = sb("consts", [P, NSHARED]), sb("cols", [P, NCOLS])
        shared.xt_hi, shared.xt_lo = (sb(n, [P, KC, T], F32R) for n in ("xt_hi", "xt_lo"))
        shared.res = sb("res", [P, TT, C])
        shared.ln_p = sb("stats_p", [P, TT, 6]), sb("mv_p", [P, TT, 2]), sb("work_p", [P, 3, TT])
        shared.x1_out, shared.xp_in, shared.ln_p_done = sem("x1_out"), sem("xp_in"), sem("ln_p_done")
        shared.xpt_done, shared.ht_done, shared.ht_parts = sem("xpt_done"), sem("ht_done"), sem("ht_parts")
        layer_a(nc, x, w_attn_a, w_out_a, consts_dram, w_qkv, cols_dram, x1, shared)
        layer_b(nc, x1, w_out_b, w_moe, rows_dram, out, shared)


def make_consts():
    f32 = np.float32
    i, j = np.arange(T)[:, None], np.arange(T)[None, :]

    def mask_rows(allowed):
        m = np.where(allowed, 0.0, MASKED)
        return np.concatenate([m[:P, :P], m[P:, :]], axis=1)

    causal = j <= i
    window = causal & ((j >= i - (WINDOW - 1)) | (j < SINK))
    inv_freq = (1.0 / f32(ROPE_THETA) ** (np.arange(0, HSB, 2, dtype=f32) / f32(HSB))).astype(f32)
    freqs = np.arange(T, dtype=f32)[:, None] * inv_freq[None, :]
    cos, sin = (np.concatenate([f(freqs), f(freqs)], axis=1).T for f in (np.cos, np.sin))
    sin = np.concatenate([-sin[:HSB // 2], sin[HSB // 2:]], axis=0)
    values = {
        "ident": np.eye(P),
        "mask_a": mask_rows(window), "mask_b": mask_rows(causal),
        "cos": cos, "sin": sin,
        "before": np.broadcast_to(np.tril(np.ones((E, E)), -1).reshape(1, E * E), (P, E * E)),
    }
    return np.ascontiguousarray(np.concatenate([values[name] for name in CONSTS], axis=1), dtype=f32)


def kernel(**inputs):
    import concourse.bacc as _bacc
    from concourse.bass_utils import run_bass_kernel_spmd as _run

    a = {name[len("L0_attn_"):]: np.asarray(v) for name, v in inputs.items() if name.startswith("L0_attn_")}
    f = {name[len("L0_ffn_"):]: np.asarray(v) for name, v in inputs.items() if name.startswith("L0_ffn_")}

    def to_partitions(v, inner):
        return np.moveaxis(v.reshape(-1, P, inner), 1, 0).reshape(P, -1)

    params = {name: to_partitions(f[name].reshape(-1, 1), 1) for name in COLS if name != "w_gate"}
    params["w_gate"] = to_partitions(f["w_gate"], E)
    wk = a["Wk"].T.reshape(C, KVA, HSA).transpose(0, 2, 1).reshape(C, KVA * HSA)
    wq = a["Wq"].T.reshape(C, C // P, HPT // 2, 2, HSA).transpose(0, 1, 4, 3, 2).reshape(C, C)
    arrays = {
        "x": a["x"],
        "w_attn_a": np.concatenate([a["Wv"].T, wk, wq], axis=1),
        "w_out_a": a["Wo"].T,
        "consts": make_consts(),
        "w_qkv": np.concatenate([to_partitions(f[name], H * HSB) for name in ("wq", "wk", "wv")], axis=1),
        "w_out_b": to_partitions(f["wo"], C),
        "w_moe": np.concatenate([to_partitions(f[name], C) for name in ("we1", "we2")], axis=1),
        "cols": np.concatenate([params[name] for name in COLS], axis=1),
        "rows": np.broadcast_to(np.concatenate([f["bo"], f["be2"].reshape(-1)])[None, :], (P, NROWS)),
    }
    arrays = {name + "_dram": np.ascontiguousarray(v) for name, v in arrays.items()}

    nc = _bacc.Bacc("TRN2", target_bir_lowering=False, num_devices=1)
    args = [nc.dram_tensor(name, v.shape, F32, kind="ExternalInput").ap() for name, v in arrays.items()]
    out = nc.dram_tensor("out_dram", (NB, T, C), F32, kind="ExternalOutput").ap()
    build(nc, *args, out)
    r = _run(nc, [arrays], core_ids=[0])
    return r.results[0]["out_dram"]
```
